# Optimizing a Trainium2 kernel written in Bass

```python
import numpy as np
import jax
import jax.numpy as jnp

def _softmax(x, axis=-1):
    return jax.nn.softmax(x, axis=axis)

def _gelu(x):
    return jax.nn.gelu(x, approximate=True)

def _silu(x):
    return jax.nn.silu(x)

def _sigmoid(x):
    return jax.nn.sigmoid(x)

def _layernorm(x, axis=-1, eps=1e-05):
    m = jnp.mean(x, axis=axis, keepdims=True)
    v = jnp.var(x, axis=axis, keepdims=True)
    return (x - m) / jnp.sqrt(v + eps)

def _scatter_add(tgt, idx, src, axis=0):
    return tgt.at[idx].add(src)

def _segment_sum(src, seg, n):
    return jax.ops.segment_sum(src, seg, n)
kernel_name = 'mk_adaln_attn_ffn_d2_seqx_r4_9964f8'

def setup_inputs(seed: int=0):
    np.random.seed(seed)
    _w = jnp.asarray

    def _rec_inputs():
        import jax
        import jax.numpy as jnp
        _rk = jax.random.key(seed)
        x = 7.22e-05 + 1 * jax.random.normal(jax.random.fold_in(_rk, 1), (2, 1024, 256), jnp.float32)
        _lenS = 1024 - jax.random.randint(jax.random.fold_in(_rk, 7), (2,), 0, max(1, 1024 // 4) + 1, jnp.int32)
        _lenS2 = 1024 - jax.random.randint(jax.random.fold_in(_rk, 8), (2,), 0, max(1, 1024 // 4) + 1, jnp.int32)
        cond_64 = -0.104238 + 1.01173 * jax.random.normal(jax.random.fold_in(_rk, 11), (2, 64), jnp.float32)
        fside_16xSxS_0 = -5.72187e-05 + 0.999849 * jax.random.normal(jax.random.fold_in(_rk, 12), (16, 1024, 1024), jnp.float32)
        _validS = jnp.arange(1024)[None, :] < _lenS[:, None]
        _validS2 = jnp.arange(1024)[None, :] < _lenS2[:, None]
        _causal = jnp.tril(jnp.ones((1024, 1024), dtype=bool))
        mask_BxS_bk0 = jnp.logical_not(jnp.broadcast_to(_validS[:, :], (2, 1024)))
        mask_BxS_bf1 = jnp.ones((2, 1024), dtype=bool)
        return (x, cond_64, fside_16xSxS_0, mask_BxS_bk0, mask_BxS_bf1)
    x, cond_64, fside_16xSxS_0, mask_BxS_bk0, mask_BxS_bf1 = _rec_inputs()

    def _L0_cond_setup():
        import jax, jax.numpy as jnp
        import numpy as np
        B, S, H = (4, 512, 256)
        E = 8
        M = 128
        K = 2
        N_SHARED = 2
        SM = M * N_SHARED
        G = 64
        GE_TEMP = 1.0
        ALPHA = 0.001
        SEQ_AUX = True
        NORM_TOPK = True
        COS_TEMP = 0.78
        CONS_ALPHA = 0.01
        LEAKY_SLOPE = 0.01
        EPS_COS = 1e-08

        def _leaky(x):
            return jnp.where(x >= 0, x, LEAKY_SLOPE * x)

        def _moe_forward(hidden_states, g, wt, wg, w_gate, w_up, w_down, sw_gate, sw_up, sw_down):
            b, s, h = hidden_states.shape
            x = hidden_states.reshape(-1, h)
            T = x.shape[0]
            logits_h = x @ wt.T
            logits_g = g @ wg.T
            logits_g = jnp.repeat(logits_g, s, axis=0)
            logits = (logits_h + logits_g / GE_TEMP) / (1.0 + 1.0 / GE_TEMP)
            scores = jax.nn.softmax(logits, axis=-1)
            topk_w, topk_idx = jax.lax.top_k(scores, K)
            if K > 1 and NORM_TOPK:
                topk_w = topk_w / (topk_w.sum(-1, keepdims=True) + 1e-20)
            onehot = jax.nn.one_hot(topk_idx.reshape(b, s * K), E, dtype=jnp.float32)
            ce = onehot.sum(1) / (s * K / E)
            aux_loss = (ce * scores.reshape(b, s, E).mean(1)).sum(1).mean() * ALPHA
            gp = _leaky(jnp.einsum('th,ehm->etm', x, w_gate))
            up = jnp.einsum('th,ehm->etm', x, w_up)
            y_all = jnp.einsum('etm,emh->eth', gp * up, w_down)
            y_sel = y_all[topk_idx, jnp.arange(T)[:, None], :]
            y = (y_sel * topk_w[..., None]).sum(1).reshape(b, s, h)
            p = _leaky(hidden_states @ sw_gate) * (hidden_states @ sw_up) @ sw_down
            y = y + p
            num = jnp.sum(y * p, -1)
            den = jnp.maximum(jnp.linalg.norm(y, axis=-1), EPS_COS) * jnp.maximum(jnp.linalg.norm(p, axis=-1), EPS_COS)
            closs = CONS_ALPHA * jnp.mean(num / den / (1.0 + COS_TEMP))
            return (y, aux_loss + closs)
        key = jax.random.key(seed)
        ks = jax.random.split(key, 12)
        sh = 1.0 / np.sqrt(H)
        sm = 1.0 / np.sqrt(M)
        ssm = 1.0 / np.sqrt(SM)
        sg = 1.0 / np.sqrt(G)
        return {'hidden_states': jax.random.normal(ks[0], (B, S, H), jnp.float32), 'g': jax.random.normal(ks[1], (B, G), jnp.float32), 'wt': jax.random.uniform(ks[2], (E, H), jnp.float32, -sh, sh), 'wg': jax.random.uniform(ks[3], (E, G), jnp.float32, -sg, sg), 'w_gate': jax.random.uniform(ks[4], (E, H, M), jnp.float32, -sh, sh), 'w_up': jax.random.uniform(ks[5], (E, H, M), jnp.float32, -sh, sh), 'w_down': jax.random.uniform(ks[6], (E, M, H), jnp.float32, -sm, sm), 'sw_gate': jax.random.uniform(ks[7], (H, SM), jnp.float32, -sh, sh), 'sw_up': jax.random.uniform(ks[8], (H, SM), jnp.float32, -sh, sh), 'sw_down': jax.random.uniform(ks[9], (SM, H), jnp.float32, -ssm, ssm)}
    _L0_cond_all = _L0_cond_setup()
    _L0_cond_in = {k: v for k, v in _L0_cond_all.items() if k in ('wt', 'wg', 'w_gate', 'w_up', 'w_down', 'sw_gate', 'sw_up', 'sw_down')}
    del _L0_cond_all

    def _L0_attn_setup():
        import jax, jax.numpy as jnp
        import numpy as np
        B, S, D, H = (2, 512, 256, 16)
        MASK_VAL = -50000.0
        key = jax.random.key(seed)
        k1, k2, k3, k4 = jax.random.split(key, 4)
        s = 1.0 / np.sqrt(D)
        return {'x': jax.random.normal(k1, (B, S, D), dtype=jnp.float32), 'Wq': jax.random.normal(k2, (D, D), dtype=jnp.float32) * s, 'Wkv': jax.random.normal(k3, (D, 2 * D), dtype=jnp.float32) * s, 'Wo': jax.random.normal(k4, (D, D), dtype=jnp.float32) * s}
    _L0_attn_all = _L0_attn_setup()
    _L0_attn_in = {k: v for k, v in _L0_attn_all.items() if k in ('Wq', 'Wkv', 'Wo')}
    del _L0_attn_all

    def _L0_cond2_setup():
        import jax, jax.numpy as jnp
        import numpy as np
        B, N, DIM, H, DH = (2, 512, 256, 16, 64)
        INNER = H * DH
        EPS = 1e-05

        def layernorm(x, g):
            mean = jnp.mean(x, axis=-1, keepdims=True)
            var = jnp.var(x, axis=-1, keepdims=True)
            return (x - mean) * jax.lax.rsqrt(var + EPS) * g
        key = jax.random.key(seed)
        ks = jax.random.split(key, 10)
        x = jax.random.normal(ks[0], (B, N, DIM), dtype=jnp.float32)
        attn_bias = jax.random.normal(ks[1], (H, N, N), dtype=jnp.float32)
        mask = jax.random.randint(ks[2], (B, N), 0, 2).astype(bool)
        g_in = jnp.ones((DIM,), dtype=jnp.float32)
        null_attn_bias = jax.random.normal(ks[3], (H,), dtype=jnp.float32)
        null_kv = jax.random.normal(ks[4], (2, DH), dtype=jnp.float32)
        Wq = jax.random.normal(ks[5], (DIM, INNER), dtype=jnp.float32) * 0.02
        Wkv = jax.random.normal(ks[6], (DIM, 2 * DH), dtype=jnp.float32) * 0.02
        Wo = jax.random.normal(ks[7], (INNER, DIM), dtype=jnp.float32) * 0.02
        g_out = jnp.ones((DIM,), dtype=jnp.float32)
        return {'x': x, 'attn_bias': attn_bias, 'mask': mask, 'g_in': g_in, 'null_attn_bias': null_attn_bias, 'null_kv': null_kv, 'Wq': Wq, 'Wkv': Wkv, 'Wo': Wo, 'g_out': g_out}
    _L0_cond2_all = _L0_cond2_setup()
    _L0_cond2_in = {k: v for k, v in _L0_cond2_all.items() if k in ('g_in', 'null_attn_bias', 'Wq', 'Wkv', 'Wo', 'g_out')}
    del _L0_cond2_all

    def _L0_ffn_setup():
        import jax, jax.numpy as jnp
        import numpy as np
        B, S, D_MODEL, D_HIDDEN = (4, 512, 256, 1024)

        def act_quant(x):
            scale = 127.0 / jnp.clip(jnp.max(jnp.abs(x), axis=-1, keepdims=True), 1e-05)
            return jnp.clip(jnp.round(x * scale), -128, 127) / scale

        def weight_quant(w):
            scale = 1.0 / jnp.clip(jnp.mean(jnp.abs(w)), 1e-05)
            return jnp.clip(jnp.round(w * scale), -1, 1) / scale

        def bit_linear(x, w):
            xq = x + jax.lax.stop_gradient(act_quant(x) - x)
            wq = w + jax.lax.stop_gradient(weight_quant(w) - w)
            return jnp.einsum('bsd,hd->bsh', xq, wq)

        def depthwise_conv1d(x_bcl, w, b):
            y = jax.lax.conv_general_dilated(x_bcl, w, window_strides=(1,), padding=[(1, 1)], dimension_numbers=('NCH', 'OIH', 'NCH'), feature_group_count=x_bcl.shape[1])
            return y + b[None, :, None]
        key = jax.random.key(seed)
        ks = jax.random.split(key, 5)
        lim1 = 1.0 / np.sqrt(D_MODEL)
        lim2 = 1.0 / np.sqrt(D_HIDDEN)
        limc = 1.0 / np.sqrt(3.0)
        return {'x': jax.random.normal(ks[0], (B, S, D_MODEL), dtype=jnp.float32), 'w1': jax.random.uniform(ks[1], (D_HIDDEN, D_MODEL), jnp.float32, -lim1, lim1), 'conv_w': jax.random.uniform(ks[2], (D_HIDDEN, 1, 3), jnp.float32, -limc, limc), 'conv_b': jax.random.uniform(ks[3], (D_HIDDEN,), jnp.float32, -limc, limc), 'w2': jax.random.uniform(ks[4], (D_MODEL, D_HIDDEN), jnp.float32, -lim2, lim2)}
    _L0_ffn_all = _L0_ffn_setup()
    _L0_ffn_in = {k: v for k, v in _L0_ffn_all.items() if k in ('w1', 'conv_w', 'conv_b', 'w2')}
    del _L0_ffn_all

    def _L1_cond_setup():
        import jax, jax.numpy as jnp
        import numpy as np
        DIM = 256
        HEADS = 16
        DIM_HEAD = 64
        SCALE = 8.0

        def ln(x, g, eps=1e-05):
            mean = x.mean(axis=-1, keepdims=True)
            var = ((x - mean) ** 2).mean(axis=-1, keepdims=True)
            return (x - mean) * jax.lax.rsqrt(var + eps) * g

        def l2norm(t):
            n = jnp.maximum(jnp.linalg.norm(t, axis=-1, keepdims=True), 1e-12)
            return t / n

        def rel_pos_bias(n, w0, b0, g0, w1, b1, g1, w2, b2, dtype):
            pos = jnp.arange(-n + 1, n, dtype=dtype)[:, None]
            h = jax.nn.silu(ln(pos @ w0 + b0, g0))
            h = jax.nn.silu(ln(h @ w1 + b1, g1))
            h = h @ w2 + b2
            i = jnp.arange(n)
            idx = i[:, None] - i[None, :] + n - 1
            bias = h[idx]
            return jnp.transpose(bias, (2, 0, 1))
        key = jax.random.key(seed)
        ks = jax.random.split(key, 16)
        b, n = (2, 512)
        inner = HEADS * DIM_HEAD
        s = 0.02
        return {'x': jax.random.normal(ks[0], (b, n, DIM), jnp.float32), 'mask': jnp.ones((b, n), dtype=bool), 'g_norm': jnp.ones((DIM,), jnp.float32), 'Wq': jax.random.normal(ks[1], (DIM, inner), jnp.float32) * s, 'Wkv': jax.random.normal(ks[2], (DIM, 2 * DIM_HEAD), jnp.float32) * s, 'q_scale': jnp.ones((DIM_HEAD,), jnp.float32), 'k_scale': jnp.ones((DIM_HEAD,), jnp.float32), 'null_kv': jax.random.normal(ks[3], (2, DIM_HEAD), jnp.float32), 'null_attn_bias': jax.random.normal(ks[4], (HEADS,), jnp.float32), 'w0': jax.random.normal(ks[5], (1, DIM), jnp.float32) * s, 'b0': jnp.zeros((DIM,), jnp.float32), 'g0': jnp.ones((DIM,), jnp.float32), 'w1': jax.random.normal(ks[6], (DIM, DIM), jnp.float32) * s, 'b1': jnp.zeros((DIM,), jnp.float32), 'g1': jnp.ones((DIM,), jnp.float32), 'w2': jax.random.normal(ks[7], (DIM, HEADS), jnp.float32) * s, 'b2': jnp.zeros((HEADS,), jnp.float32), 'Wout': jax.random.normal(ks[8], (inner, DIM), jnp.float32) * s, 'g_out': jnp.ones((DIM,), jnp.float32)}
    _L1_cond_all = _L1_cond_setup()
    _L1_cond_in = {k: v for k, v in _L1_cond_all.items() if k in ('g_norm', 'Wq', 'Wkv', 'q_scale', 'k_scale', 'null_attn_bias', 'w0', 'b0', 'g0', 'w1', 'b1', 'g1', 'w2', 'b2', 'Wout', 'g_out')}
    del _L1_cond_all

    def _L1_attn_setup():
        import jax, jax.numpy as jnp
        import numpy as np
        D_K = 128
        key = jax.random.key(seed)
        ks = jax.random.split(key, 5)
        B, T, D = (4, 512, 256)
        scale = 0.02
        return {'x': jax.random.normal(ks[0], (B, T, D), dtype=jnp.float32), 'Wq': jax.random.normal(ks[1], (D, D_K), dtype=jnp.float32) * scale, 'Wk': jax.random.normal(ks[2], (D, D_K), dtype=jnp.float32) * scale, 'Wv': jax.random.normal(ks[3], (D, D_K), dtype=jnp.float32) * scale, 'Wo': jax.random.normal(ks[4], (D_K, D), dtype=jnp.float32) * scale}
    _L1_attn_all = _L1_attn_setup()
    _L1_attn_in = {k: v for k, v in _L1_attn_all.items() if k in ('Wq', 'Wk', 'Wv', 'Wo')}
    del _L1_attn_all

    def _L1_cond2_setup():
        import jax, jax.numpy as jnp
        import numpy as np
        B, N, DIM, H, DH = (2, 512, 256, 16, 64)
        INNER = H * DH
        EPS = 1e-05

        def layernorm(x, g):
            mean = jnp.mean(x, axis=-1, keepdims=True)
            var = jnp.var(x, axis=-1, keepdims=True)
            return (x - mean) * jax.lax.rsqrt(var + EPS) * g
        key = jax.random.key(seed)
        ks = jax.random.split(key, 10)
        x = jax.random.normal(ks[0], (B, N, DIM), dtype=jnp.float32)
        attn_bias = jax.random.normal(ks[1], (H, N, N), dtype=jnp.float32)
        mask = jax.random.randint(ks[2], (B, N), 0, 2).astype(bool)
        g_in = jnp.ones((DIM,), dtype=jnp.float32)
        null_attn_bias = jax.random.normal(ks[3], (H,), dtype=jnp.float32)
        null_kv = jax.random.normal(ks[4], (2, DH), dtype=jnp.float32)
        Wq = jax.random.normal(ks[5], (DIM, INNER), dtype=jnp.float32) * 0.02
        Wkv = jax.random.normal(ks[6], (DIM, 2 * DH), dtype=jnp.float32) * 0.02
        Wo = jax.random.normal(ks[7], (INNER, DIM), dtype=jnp.float32) * 0.02
        g_out = jnp.ones((DIM,), dtype=jnp.float32)
        return {'x': x, 'attn_bias': attn_bias, 'mask': mask, 'g_in': g_in, 'null_attn_bias': null_attn_bias, 'null_kv': null_kv, 'Wq': Wq, 'Wkv': Wkv, 'Wo': Wo, 'g_out': g_out}
    _L1_cond2_all = _L1_cond2_setup()
    _L1_cond2_in = {k: v for k, v in _L1_cond2_all.items() if k in ('g_in', 'null_attn_bias', 'Wq', 'Wkv', 'Wo', 'g_out')}
    del _L1_cond2_all

    def _L1_ffn_setup():
        import jax, jax.numpy as jnp
        import numpy as np
        B, T, D, F, E = (2, 512, 256, 1024, 8)
        TOP_K = 2
        key = jax.random.key(seed)
        k0, k1, k2, k3 = jax.random.split(key, 4)
        x = jax.random.normal(k0, (B, T, D), dtype=jnp.float32)
        Wr = jax.random.normal(k1, (D, E), dtype=jnp.float32) * 0.02
        W1 = jax.random.normal(k2, (E, D, F), dtype=jnp.float32) * 0.02
        b1 = jnp.zeros((E, F), dtype=jnp.float32)
        W2 = jax.random.normal(k3, (E, F, D), dtype=jnp.float32) * 0.02
        b2 = jnp.zeros((E, D), dtype=jnp.float32)
        return {'x': x, 'Wr': Wr, 'W1': W1, 'b1': b1, 'W2': W2, 'b2': b2}
    _L1_ffn_all = _L1_ffn_setup()
    _L1_ffn_in = {k: v for k, v in _L1_ffn_all.items() if k in ('Wr', 'W1', 'b1', 'W2', 'b2')}
    del _L1_ffn_all
    return {'x': x, 'cond_64': cond_64, 'fside_16xSxS_0': fside_16xSxS_0, 'mask_BxS_bk0': mask_BxS_bk0, 'mask_BxS_bf1': mask_BxS_bf1, 'L0_cond_wt': _L0_cond_in['wt'], 'L0_cond_wg': _L0_cond_in['wg'], 'L0_cond_w_gate': _L0_cond_in['w_gate'], 'L0_cond_w_up': _L0_cond_in['w_up'], 'L0_cond_w_down': _L0_cond_in['w_down'], 'L0_cond_sw_gate': _L0_cond_in['sw_gate'], 'L0_cond_sw_up': _L0_cond_in['sw_up'], 'L0_cond_sw_down': _L0_cond_in['sw_down'], 'L0_attn_Wq': _L0_attn_in['Wq'], 'L0_attn_Wkv': _L0_attn_in['Wkv'], 'L0_attn_Wo': _L0_attn_in['Wo'], 'L0_cond2_g_in': _L0_cond2_in['g_in'], 'L0_cond2_null_attn_bias': _L0_cond2_in['null_attn_bias'], 'L0_cond2_Wq': _L0_cond2_in['Wq'], 'L0_cond2_Wkv': _L0_cond2_in['Wkv'], 'L0_cond2_Wo': _L0_cond2_in['Wo'], 'L0_cond2_g_out': _L0_cond2_in['g_out'], 'L0_ffn_w1': _L0_ffn_in['w1'], 'L0_ffn_conv_w': _L0_ffn_in['conv_w'], 'L0_ffn_conv_b': _L0_ffn_in['conv_b'], 'L0_ffn_w2': _L0_ffn_in['w2'], 'L1_cond_g_norm': _L1_cond_in['g_norm'], 'L1_cond_Wq': _L1_cond_in['Wq'], 'L1_cond_Wkv': _L1_cond_in['Wkv'], 'L1_cond_q_scale': _L1_cond_in['q_scale'], 'L1_cond_k_scale': _L1_cond_in['k_scale'], 'L1_cond_null_attn_bias': _L1_cond_in['null_attn_bias'], 'L1_cond_w0': _L1_cond_in['w0'], 'L1_cond_b0': _L1_cond_in['b0'], 'L1_cond_g0': _L1_cond_in['g0'], 'L1_cond_w1': _L1_cond_in['w1'], 'L1_cond_b1': _L1_cond_in['b1'], 'L1_cond_g1': _L1_cond_in['g1'], 'L1_cond_w2': _L1_cond_in['w2'], 'L1_cond_b2': _L1_cond_in['b2'], 'L1_cond_Wout': _L1_cond_in['Wout'], 'L1_cond_g_out': _L1_cond_in['g_out'], 'L1_attn_Wq': _L1_attn_in['Wq'], 'L1_attn_Wk': _L1_attn_in['Wk'], 'L1_attn_Wv': _L1_attn_in['Wv'], 'L1_attn_Wo': _L1_attn_in['Wo'], 'L1_cond2_g_in': _L1_cond2_in['g_in'], 'L1_cond2_null_attn_bias': _L1_cond2_in['null_attn_bias'], 'L1_cond2_Wq': _L1_cond2_in['Wq'], 'L1_cond2_Wkv': _L1_cond2_in['Wkv'], 'L1_cond2_Wo': _L1_cond2_in['Wo'], 'L1_cond2_g_out': _L1_cond2_in['g_out'], 'L1_ffn_Wr': _L1_ffn_in['Wr'], 'L1_ffn_W1': _L1_ffn_in['W1'], 'L1_ffn_b1': _L1_ffn_in['b1'], 'L1_ffn_W2': _L1_ffn_in['W2'], 'L1_ffn_b2': _L1_ffn_in['b2']}

def reference(x, cond_64, fside_16xSxS_0, mask_BxS_bk0, mask_BxS_bf1, L0_cond_wt, L0_cond_wg, L0_cond_w_gate, L0_cond_w_up, L0_cond_w_down, L0_cond_sw_gate, L0_cond_sw_up, L0_cond_sw_down, L0_attn_Wq, L0_attn_Wkv, L0_attn_Wo, L0_cond2_g_in, L0_cond2_null_attn_bias, L0_cond2_Wq, L0_cond2_Wkv, L0_cond2_Wo, L0_cond2_g_out, L0_ffn_w1, L0_ffn_conv_w, L0_ffn_conv_b, L0_ffn_w2, L1_cond_g_norm, L1_cond_Wq, L1_cond_Wkv, L1_cond_q_scale, L1_cond_k_scale, L1_cond_null_attn_bias, L1_cond_w0, L1_cond_b0, L1_cond_g0, L1_cond_w1, L1_cond_b1, L1_cond_g1, L1_cond_w2, L1_cond_b2, L1_cond_Wout, L1_cond_g_out, L1_attn_Wq, L1_attn_Wk, L1_attn_Wv, L1_attn_Wo, L1_cond2_g_in, L1_cond2_null_attn_bias, L1_cond2_Wq, L1_cond2_Wkv, L1_cond2_Wo, L1_cond2_g_out, L1_ffn_Wr, L1_ffn_W1, L1_ffn_b1, L1_ffn_W2, L1_ffn_b2):
    import jax
    import jax.numpy as jnp

    def _L0_cond_ref(hidden_states, g, wt, wg, w_gate, w_up, w_down, sw_gate, sw_up, sw_down):
        import jax, jax.numpy as jnp
        import numpy as np
        B, S, H = (4, 512, 256)
        E = 8
        M = 128
        K = 2
        N_SHARED = 2
        SM = M * N_SHARED
        G = 64
        GE_TEMP = 1.0
        ALPHA = 0.001
        SEQ_AUX = True
        NORM_TOPK = True
        COS_TEMP = 0.78
        CONS_ALPHA = 0.01
        LEAKY_SLOPE = 0.01
        EPS_COS = 1e-08

        def _leaky(x):
            return jnp.where(x >= 0, x, LEAKY_SLOPE * x)

        def _moe_forward(hidden_states, g, wt, wg, w_gate, w_up, w_down, sw_gate, sw_up, sw_down):
            b, s, h = hidden_states.shape
            x = hidden_states.reshape(-1, h)
            T = x.shape[0]
            logits_h = x @ wt.T
            logits_g = g @ wg.T
            logits_g = jnp.repeat(logits_g, s, axis=0)
            logits = (logits_h + logits_g / GE_TEMP) / (1.0 + 1.0 / GE_TEMP)
            scores = jax.nn.softmax(logits, axis=-1)
            topk_w, topk_idx = jax.lax.top_k(scores, K)
            if K > 1 and NORM_TOPK:
                topk_w = topk_w / (topk_w.sum(-1, keepdims=True) + 1e-20)
            onehot = jax.nn.one_hot(topk_idx.reshape(b, s * K), E, dtype=jnp.float32)
            ce = onehot.sum(1) / (s * K / E)
            aux_loss = (ce * scores.reshape(b, s, E).mean(1)).sum(1).mean() * ALPHA
            gp = _leaky(jnp.einsum('th,ehm->etm', x, w_gate))
            up = jnp.einsum('th,ehm->etm', x, w_up)
            y_all = jnp.einsum('etm,emh->eth', gp * up, w_down)
            y_sel = y_all[topk_idx, jnp.arange(T)[:, None], :]
            y = (y_sel * topk_w[..., None]).sum(1).reshape(b, s, h)
            p = _leaky(hidden_states @ sw_gate) * (hidden_states @ sw_up) @ sw_down
            y = y + p
            num = jnp.sum(y * p, -1)
            den = jnp.maximum(jnp.linalg.norm(y, axis=-1), EPS_COS) * jnp.maximum(jnp.linalg.norm(p, axis=-1), EPS_COS)
            closs = CONS_ALPHA * jnp.mean(num / den / (1.0 + COS_TEMP))
            return (y, aux_loss + closs)
        y, _ = _moe_forward(hidden_states, g, wt, wg, w_gate, w_up, w_down, sw_gate, sw_up, sw_down)
        return y

    def _L0_attn_ref(x, Wq, Wkv, Wo):
        import jax, jax.numpy as jnp
        import numpy as np
        B, S, D, H = (2, 512, 256, 16)
        MASK_VAL = -50000.0
        b, sl, d = x.shape
        h = H
        hd = d // h
        scale = hd ** (-0.5)
        q = x @ Wq
        kv = x @ Wkv
        k, v = jnp.split(kv, 2, axis=-1)
        q = q.reshape(b, sl, h, hd).transpose(0, 2, 1, 3)
        k = k.reshape(b, sl, h, hd).transpose(0, 2, 1, 3)
        v = v.reshape(b, sl, h, hd).transpose(0, 2, 1, 3)
        dots = jnp.einsum('bhid,bhjd->bhij', q * scale, k)
        causal = jnp.tril(jnp.ones((sl, sl), dtype=bool))
        dots = jnp.where(causal, dots, MASK_VAL)
        attn = jax.nn.softmax(dots, axis=-1)
        out = jnp.einsum('bhij,bhjd->bihd', attn, v).reshape(b, sl, d)
        return out @ Wo

    def _L0_cond2_ref(x, attn_bias, mask, g_in, null_attn_bias, null_kv, Wq, Wkv, Wo, g_out):
        import jax, jax.numpy as jnp
        import numpy as np
        B, N, DIM, H, DH = (2, 512, 256, 16, 64)
        INNER = H * DH
        EPS = 1e-05

        def layernorm(x, g):
            mean = jnp.mean(x, axis=-1, keepdims=True)
            var = jnp.var(x, axis=-1, keepdims=True)
            return (x - mean) * jax.lax.rsqrt(var + EPS) * g
        b, n, _ = x.shape
        scale = DH ** (-0.5)
        xn = layernorm(x, g_in)
        q = (xn @ Wq).reshape(b, n, H, DH).transpose(0, 2, 1, 3) * scale
        kv = xn @ Wkv
        k, v = (kv[..., :DH], kv[..., DH:])
        nk = jnp.broadcast_to(null_kv[0], (b, 1, DH))
        nv = jnp.broadcast_to(null_kv[1], (b, 1, DH))
        k = jnp.concatenate([nk, k], axis=1)
        v = jnp.concatenate([nv, v], axis=1)
        sim = jnp.einsum('bhid,bjd->bhij', q, k)
        null_col = jnp.broadcast_to(null_attn_bias[:, None, None], (H, n, 1))
        bias = jnp.concatenate([null_col, attn_bias], axis=-1)
        sim = sim + bias
        neg = -jnp.finfo(sim.dtype).max
        j = n + 1
        causal_mask = jnp.triu(jnp.ones((n, j), dtype=bool), k=j - n + 1)
        sim = jnp.where(causal_mask, neg, sim)
        mask_p = jnp.pad(mask, ((0, 0), (1, 0)), constant_values=True)
        sim = jnp.where(mask_p[:, None, None, :], sim, neg)
        attn = jax.nn.softmax(sim, axis=-1)
        out = jnp.einsum('bhij,bjd->bhid', attn, v)
        out = out.transpose(0, 2, 1, 3).reshape(b, n, INNER)
        out = out @ Wo
        return layernorm(out, g_out)

    def _L0_ffn_ref(x, w1, conv_w, conv_b, w2):
        import jax, jax.numpy as jnp
        import numpy as np
        B, S, D_MODEL, D_HIDDEN = (4, 512, 256, 1024)

        def act_quant(x):
            scale = 127.0 / jnp.clip(jnp.max(jnp.abs(x), axis=-1, keepdims=True), 1e-05)
            return jnp.clip(jnp.round(x * scale), -128, 127) / scale

        def weight_quant(w):
            scale = 1.0 / jnp.clip(jnp.mean(jnp.abs(w)), 1e-05)
            return jnp.clip(jnp.round(w * scale), -1, 1) / scale

        def bit_linear(x, w):
            xq = x + jax.lax.stop_gradient(act_quant(x) - x)
            wq = w + jax.lax.stop_gradient(weight_quant(w) - w)
            return jnp.einsum('bsd,hd->bsh', xq, wq)

        def depthwise_conv1d(x_bcl, w, b):
            y = jax.lax.conv_general_dilated(x_bcl, w, window_strides=(1,), padding=[(1, 1)], dimension_numbers=('NCH', 'OIH', 'NCH'), feature_group_count=x_bcl.shape[1])
            return y + b[None, :, None]
        h = bit_linear(x, w1)
        h = depthwise_conv1d(h.transpose(0, 2, 1), conv_w, conv_b)
        h = h.transpose(0, 2, 1)
        h = jax.nn.silu(h)
        return bit_linear(h, w2)

    def _L1_cond_ref(x, mask, g_norm, Wq, Wkv, q_scale, k_scale, null_kv, null_attn_bias, w0, b0, g0, w1, b1, g1, w2, b2, Wout, g_out):
        import jax, jax.numpy as jnp
        import numpy as np
        DIM = 256
        HEADS = 16
        DIM_HEAD = 64
        SCALE = 8.0

        def ln(x, g, eps=1e-05):
            mean = x.mean(axis=-1, keepdims=True)
            var = ((x - mean) ** 2).mean(axis=-1, keepdims=True)
            return (x - mean) * jax.lax.rsqrt(var + eps) * g

        def l2norm(t):
            n = jnp.maximum(jnp.linalg.norm(t, axis=-1, keepdims=True), 1e-12)
            return t / n

        def rel_pos_bias(n, w0, b0, g0, w1, b1, g1, w2, b2, dtype):
            pos = jnp.arange(-n + 1, n, dtype=dtype)[:, None]
            h = jax.nn.silu(ln(pos @ w0 + b0, g0))
            h = jax.nn.silu(ln(h @ w1 + b1, g1))
            h = h @ w2 + b2
            i = jnp.arange(n)
            idx = i[:, None] - i[None, :] + n - 1
            bias = h[idx]
            return jnp.transpose(bias, (2, 0, 1))
        b, n, _ = x.shape
        xn = ln(x, g_norm)
        q = (xn @ Wq).reshape(b, n, HEADS, DIM_HEAD).transpose(0, 2, 1, 3)
        kv = xn @ Wkv
        k, v = (kv[..., :DIM_HEAD], kv[..., DIM_HEAD:])
        nk = jnp.broadcast_to(null_kv[0], (b, 1, DIM_HEAD))
        nv = jnp.broadcast_to(null_kv[1], (b, 1, DIM_HEAD))
        k = jnp.concatenate([nk, k], axis=1)
        v = jnp.concatenate([nv, v], axis=1)
        q = l2norm(q) * q_scale
        k = l2norm(k) * k_scale
        sim = jnp.einsum('bhid,bjd->bhij', q, k) * SCALE
        bias = rel_pos_bias(n, w0, b0, g0, w1, b1, g1, w2, b2, q.dtype)
        null_bias = jnp.broadcast_to(null_attn_bias[:, None, None], (HEADS, n, 1))
        attn_bias = jnp.concatenate([null_bias, bias], axis=-1)
        sim = sim + attn_bias
        neg = -jnp.finfo(sim.dtype).max
        causal = jnp.triu(jnp.ones((n, n + 1), dtype=bool), k=2)
        sim = jnp.where(causal, neg, sim)
        m = jnp.pad(mask, ((0, 0), (1, 0)), constant_values=True)[:, None, None, :]
        sim = jnp.where(m, sim, neg)
        attn = jax.nn.softmax(sim, axis=-1)
        out = jnp.einsum('bhij,bjd->bhid', attn, v)
        out = out.transpose(0, 2, 1, 3).reshape(b, n, HEADS * DIM_HEAD)
        return ln(out @ Wout, g_out)

    def _L1_attn_ref(x, Wq, Wk, Wv, Wo):
        import jax, jax.numpy as jnp
        import numpy as np
        D_K = 128
        Q = x @ Wq
        K = x @ Wk
        V = x @ Wv
        d_k = Q.shape[-1]
        logits = jnp.einsum('bqd,bkd->bqk', Q, K) * d_k ** (-0.5)
        T = logits.shape[-1]
        causal = jnp.triu(jnp.ones((T, T), dtype=bool), k=1)
        logits = jnp.where(causal, -jnp.inf, logits)
        attn = jax.nn.softmax(logits, axis=-1)
        out = jnp.einsum('bqk,bkd->bqd', attn, V)
        return out @ Wo

    def _L1_cond2_ref(x, attn_bias, mask, g_in, null_attn_bias, null_kv, Wq, Wkv, Wo, g_out):
        import jax, jax.numpy as jnp
        import numpy as np
        B, N, DIM, H, DH = (2, 512, 256, 16, 64)
        INNER = H * DH
        EPS = 1e-05

        def layernorm(x, g):
            mean = jnp.mean(x, axis=-1, keepdims=True)
            var = jnp.var(x, axis=-1, keepdims=True)
            return (x - mean) * jax.lax.rsqrt(var + EPS) * g
        b, n, _ = x.shape
        scale = DH ** (-0.5)
        xn = layernorm(x, g_in)
        q = (xn @ Wq).reshape(b, n, H, DH).transpose(0, 2, 1, 3) * scale
        kv = xn @ Wkv
        k, v = (kv[..., :DH], kv[..., DH:])
        nk = jnp.broadcast_to(null_kv[0], (b, 1, DH))
        nv = jnp.broadcast_to(null_kv[1], (b, 1, DH))
        k = jnp.concatenate([nk, k], axis=1)
        v = jnp.concatenate([nv, v], axis=1)
        sim = jnp.einsum('bhid,bjd->bhij', q, k)
        null_col = jnp.broadcast_to(null_attn_bias[:, None, None], (H, n, 1))
        bias = jnp.concatenate([null_col, attn_bias], axis=-1)
        sim = sim + bias
        neg = -jnp.finfo(sim.dtype).max
        j = n + 1
        causal_mask = jnp.triu(jnp.ones((n, j), dtype=bool), k=j - n + 1)
        sim = jnp.where(causal_mask, neg, sim)
        mask_p = jnp.pad(mask, ((0, 0), (1, 0)), constant_values=True)
        sim = jnp.where(mask_p[:, None, None, :], sim, neg)
        attn = jax.nn.softmax(sim, axis=-1)
        out = jnp.einsum('bhij,bjd->bhid', attn, v)
        out = out.transpose(0, 2, 1, 3).reshape(b, n, INNER)
        out = out @ Wo
        return layernorm(out, g_out)

    def _L1_ffn_ref(x, Wr, W1, b1, W2, b2):
        import jax, jax.numpy as jnp
        import numpy as np
        B, T, D, F, E = (2, 512, 256, 1024, 8)
        TOP_K = 2
        logits = jnp.einsum('btd,de->bte', x, Wr)
        probs = jax.nn.softmax(logits, axis=-1)
        top_v, top_i = jax.lax.top_k(probs, TOP_K)
        top_v = top_v / jnp.sum(top_v, axis=-1, keepdims=True)
        combine = jnp.sum(jax.nn.one_hot(top_i, E, dtype=x.dtype) * top_v[..., None], axis=-2)
        h = jax.nn.gelu(jnp.einsum('btd,edf->ebtf', x, W1) + b1[:, None, None, :], approximate=False)
        y = jnp.einsum('ebtf,efd->ebtd', h, W2) + b2[:, None, None, :]
        out = jnp.einsum('ebtd,bte->btd', y, combine)
        return out
    x = x + _L0_attn_ref(_L0_cond_ref(x, cond_64, L0_cond_wt, L0_cond_wg, L0_cond_w_gate, L0_cond_w_up, L0_cond_w_down, L0_cond_sw_gate, L0_cond_sw_up, L0_cond_sw_down), L0_attn_Wq, L0_attn_Wkv, L0_attn_Wo)
    x = x + _L0_ffn_ref(_L0_cond2_ref(x, fside_16xSxS_0, mask_BxS_bk0, L0_cond2_g_in, L0_cond2_null_attn_bias, cond_64, L0_cond2_Wq, L0_cond2_Wkv, L0_cond2_Wo, L0_cond2_g_out), L0_ffn_w1, L0_ffn_conv_w, L0_ffn_conv_b, L0_ffn_w2)
    x = x + _L1_attn_ref(_L1_cond_ref(x, mask_BxS_bf1, L1_cond_g_norm, L1_cond_Wq, L1_cond_Wkv, L1_cond_q_scale, L1_cond_k_scale, cond_64, L1_cond_null_attn_bias, L1_cond_w0, L1_cond_b0, L1_cond_g0, L1_cond_w1, L1_cond_b1, L1_cond_g1, L1_cond_w2, L1_cond_b2, L1_cond_Wout, L1_cond_g_out), L1_attn_Wq, L1_attn_Wk, L1_attn_Wv, L1_attn_Wo)
    x = x + _L1_ffn_ref(_L1_cond2_ref(x, fside_16xSxS_0, mask_BxS_bk0, L1_cond2_g_in, L1_cond2_null_attn_bias, cond_64, L1_cond2_Wq, L1_cond2_Wkv, L1_cond2_Wo, L1_cond2_g_out), L1_ffn_Wr, L1_ffn_W1, L1_ffn_b1, L1_ffn_W2, L1_ffn_b2)
    return x

_drawn_inputs = setup_inputs


def setup_inputs(seed=0):
    import zlib

    import numpy as np

    out = dict(_drawn_inputs(seed))
    spreads = {'L0_cond2_g_in': (1.0, 0.6),
     'L0_cond2_g_out': (1.0, 0.6),
     'L1_cond_g_norm': (1.0, 0.6),
     'L1_cond_q_scale': (1.0, 0.6),
     'L1_cond_k_scale': (1.0, 0.6),
     'L1_cond_b0': (0.0, 2.0),
     'L1_cond_g0': (1.0, 0.6),
     'L1_cond_b1': (0.0, 2.0),
     'L1_cond_g1': (1.0, 0.6),
     'L1_cond_b2': (0.0, 2.0),
     'L1_cond_g_out': (1.0, 0.6),
     'L1_cond2_g_in': (1.0, 0.6),
     'L1_cond2_g_out': (1.0, 0.6),
     'L1_ffn_b1': (0.0, 2.0),
     'L1_ffn_b2': (0.0, 0.8)}
    factors = {'L0_cond_wt': 7.425,
     'L0_cond_wg': 7.428,
     'L0_cond_w_gate': 5.675,
     'L0_cond_w_up': 5.144,
     'L0_cond_w_down': 4.796,
     'L0_cond_sw_gate': 4.123,
     'L0_cond_sw_up': 3.716,
     'L0_cond_sw_down': 3.701,
     'L0_attn_Wq': 8.0,
     'L0_attn_Wkv': 2.847,
     'L0_attn_Wo': 3.074,
     'L0_cond2_null_attn_bias': 37.624,
     'L0_cond2_Wq': 64.0,
     'L0_cond2_Wkv': 21.488,
     'L1_cond_Wq': 64.0,
     'L1_cond_null_attn_bias': 32.968,
     'L1_cond_w0': 64.0,
     'L1_cond_w1': 64.0,
     'L1_cond_w2': 64.0,
     'L1_attn_Wq': 64.0,
     'L1_attn_Wk': 64.0,
     'L1_cond2_null_attn_bias': 25.872,
     'L1_cond2_Wq': 37.776,
     'fside_16xSxS_0': 8.0,
     'L0_cond2_Wo': 8.0,
     'L0_ffn_w1': 8.0,
     'L0_ffn_conv_w': 8.0,
     'L0_ffn_conv_b': 8.0,
     'L0_ffn_w2': 8.0,
     'L1_cond_Wkv': 8.0,
     'L1_cond_Wout': 8.0,
     'L1_attn_Wv': 8.0,
     'L1_attn_Wo': 8.0,
     'L1_cond2_Wkv': 8.0,
     'L1_cond2_Wo': 8.0,
     'L1_ffn_Wr': 8.0,
     'L1_ffn_W1': 8.0,
     'L1_ffn_W2': 8.0}
    for name, (base, spread) in spreads.items():
        noise = np.random.default_rng([zlib.crc32(name.encode()), seed]).standard_normal(out[name].shape)
        drawn = base * np.exp(spread * noise) if base else spread * noise
        out[name] = jnp.asarray(drawn.astype(out[name].dtype))
    for name, factor in factors.items():
        out[name] = (out[name] * factor).astype(out[name].dtype)
    return out
```

```python
from contextlib import ExitStack, contextmanager

import numpy as np

import concourse.bass as bass
from concourse import mybir

F32 = mybir.dt.float32
BF16 = mybir.dt.bfloat16
U32 = mybir.dt.uint32
U8 = mybir.dt.uint8
ALU = mybir.AluOpType
ACT = mybir.ActivationFunctionType
AX = mybir.AxisListType

P = 128
B, S, D = 2, 1024, 256
NT = B * S // P
QB = S // P
DC = D // P
GRP = 512
NG = B * S // GRP
FAR = -1.0e38
EPS = 1e-5
ROUND = 1.5 * 2.0 ** 23


class Parts:
    pass


def loop(engine, n):
    if n == 1:
        @contextmanager
        def once():
            yield 0
        return once()
    return engine.Fori(0, n)


def hold(engine, taken):
    engine.sem_inc(taken, 1)


def turn_tensor(nc, pe, m, src, turned, freed, ready=None, tiles_ready=1, n_tiles=NT):
    for g in range(n_tiles // 4):
        if ready is not None:
            pe.wait_ge(ready, tiles_ready * (g + 1))
        for c in range(DC):
            j = DC * g + c
            if j >= 2:
                pe.wait_ge(freed, j - 1)
            for t in range(4):
                last = nc.tensor.transpose(m.T[c][:, t * P:(t + 1) * P],
                                           src[:, 4 * g + t, c * P:(c + 1) * P], m.ident[:, :])
            last.then_inc(turned, 1)


def turn_scalar(nc, act, m, dst, turned, freed, n_tiles=NT):
    for g in range(n_tiles // 4):
        for c in range(DC):
            act.wait_ge(turned, DC * g + c + 1)
            nc.scalar.copy(dst[:, c, g * GRP:(g + 1) * GRP], m.T[c][:, :]).then_inc(freed, 1)


def norm_vector(nc, dve, k, src, dst, g_row, sem, rooted, out_ready, n_tiles=NT):
    for t in range(n_tiles):
        nc.vector.bn_stats(k.bn[:, t, :], src[:, t, :]).then_inc(sem, 1)
    for t in range(n_tiles):
        dve.wait_ge(sem, t + 1)
        nc.vector.bn_aggr(k.mv[:, t, :], k.bn[:, t, :]).then_inc(sem, 1)
    n = 2 * n_tiles
    dve.wait_ge(sem, n)
    nc.vector.tensor_scalar(k.std[:, 0:n_tiles], k.mv[:, 0:n_tiles, 1], EPS, None, ALU.add).then_inc(sem, 1)
    dve.wait_ge(rooted, 1)
    nc.vector.reciprocal(k.rstd[:, 0:n_tiles], k.std[:, 0:n_tiles]).then_inc(sem, 1)
    n += 2
    dve.wait_ge(sem, n)
    for t in range(n_tiles):
        nc.vector.tensor_scalar(dst[:, t, :], src[:, t, :], k.mv[:, t, 0:1], k.rstd[:, t:t + 1],
                                ALU.subtract, ALU.mult).then_inc(sem, 1)
        dve.wait_ge(sem, n + t + 1)
        nc.vector.tensor_tensor(dst[:, t, :], dst[:, t, :], g_row[:, :], ALU.mult).then_inc(out_ready, 1)


def norm_scalar(nc, act, k, sem, rooted, n_tiles=NT):
    act.wait_ge(sem, 2 * n_tiles + 1)
    nc.scalar.activation(k.std[:, 0:n_tiles], k.std[:, 0:n_tiles], ACT.Sqrt).then_inc(rooted, 1)


def norm_buffers(m, at, name):
    k = Parts()
    k.bn = m.sb(name + "_bn", [P, NT, 6], F32, at)
    k.mv = m.sb(name + "_mv", [P, NT, 2], F32, at + 384)
    k.std = m.sb(name + "_std", [P, NT], F32, at + 512)
    k.rstd = m.sb(name + "_rstd", [P, NT], F32, at + 576)
    return k


NORM_BYTES = 640


def stage_norm_turn(nc, m, name, src, dst, xt, g_row, g_ready, at, n_tiles=NT, silu=False):
    k = norm_buffers(m, at, name)
    steps, rooted, normed, smooth, turned, freed = (m.sem(f"{name}_{s}") for s in
                                                    ("steps", "rooted", "normed", "smooth", "turned", "freed"))
    with nc.Block() as block:
        @block.vector
        def _(dve):
            dve.wait_ge(*g_ready)
            norm_vector(nc, dve, k, src, dst, g_row, steps, rooted, normed, n_tiles)

        @block.scalar
        def _(act):
            norm_scalar(nc, act, k, steps, rooted, n_tiles)
            if silu:
                for t in range(n_tiles):
                    act.wait_ge(normed, t + 1)
                    nc.scalar.activation(dst[:, t, :], dst[:, t, :], ACT.Silu).then_inc(smooth, 1)
            if xt is not None:
                turn_scalar(nc, act, m, xt, turned, freed, n_tiles)

        if xt is not None:
            @block.tensor
            def _(pe):
                turn_tensor(nc, pe, m, dst, turned, freed, smooth if silu else normed, 4, n_tiles)


def stage_turn(nc, m, name, src, xt):
    turned, freed = m.sem(name + "_turned"), m.sem(name + "_freed")
    with nc.Block() as block:
        @block.tensor
        def _(pe):
            turn_tensor(nc, pe, m, src, turned, freed)

        @block.scalar
        def _(act):
            turn_scalar(nc, act, m, xt, turned, freed)


def stage_setup(nc, m, d):
    loaded, made = m.sem("setup_loaded"), m.sem("setup_made")
    with nc.Block() as block:
        @block.sync
        def _(sp):
            sp.dma_start(m.X[:, :, :], d["x"].rearrange("b (t p) d -> p (b t) d", p=P)).then_inc(loaded, 16)
            sp.wait_ge(loaded, 16)

        @block.gpsimd
        def _(pool):
            nc.gpsimd.memset(m.ident[:, :], 0.0).then_inc(made, 1)
            nc.gpsimd.memset(m.ones[:, :], 1.0).then_inc(made, 1)
            pool.wait_ge(made, 2)
            nc.gpsimd.affine_select(out=m.ident[:, :], in_=m.ident[:, :], compare_op=ALU.not_equal, fill=1.0,
                                    base=0, pattern=[[-1, P]], channel_multiplier=1).then_inc(made, 1)
            pool.wait_ge(made, 3)
            nc.gpsimd.tensor_copy(m.identb[:, :], m.ident[:, :]).then_inc(made, 1)


def route_vector(nc, dve, m, k, logits, scale, tiny, E, sem, exped):
    cnt = [0]

    def step(ins):
        cnt[0] += 1
        ins.then_inc(sem, 1)
        dve.wait_ge(sem, cnt[0])

    wide = [P, NT, E]
    step(nc.vector.tensor_scalar(k.l[:, :, :], logits, scale, None, ALU.mult))
    step(nc.vector.tensor_reduce(k.mx[:, :], k.l[:, :, :], AX.X, ALU.max))
    step(nc.vector.tensor_tensor(k.l[:, :, :], k.l[:, :, :], k.mx[:, :].unsqueeze(2).broadcast_to(wide),
                                 ALU.subtract))
    dve.wait_ge(exped, 1)
    step(nc.vector.tensor_reduce(k.mx[:, :], k.l[:, :, :], AX.X, ALU.add))
    step(nc.vector.reciprocal(k.mx[:, :], k.mx[:, :]))
    step(nc.vector.tensor_tensor(k.l[:, :, :], k.l[:, :, :], k.mx[:, :].unsqueeze(2).broadcast_to(wide),
                                 ALU.mult))
    for t in range(NT):
        last = nc.vector.max(k.top[:, t, :], k.l[:, t, :])
    step(last)
    for t in range(NT):
        last = nc.vector.max_index(k.idx[:, t, :], k.top[:, t, :], k.l[:, t, :])
    step(last)
    step(nc.vector.tensor_copy(k.idxf[:, :, :], k.idx[:, :, 0:2]))
    step(nc.vector.tensor_tensor(k.mx[:, :], k.top[:, :, 0], k.top[:, :, 1], ALU.add))
    step(nc.vector.tensor_scalar(k.mx[:, :], k.mx[:, :], tiny, None, ALU.add))
    step(nc.vector.reciprocal(k.mx[:, :], k.mx[:, :]))
    step(nc.vector.tensor_tensor(k.w2[:, :, :], k.top[:, :, 0:2],
                                 k.mx[:, :].unsqueeze(2).broadcast_to([P, NT, 2]), ALU.mult))
    number = k.iota[:, 0:E].unsqueeze(1).broadcast_to(wide)
    for c, hot in enumerate((k.l, k.hot)):
        step(nc.vector.tensor_tensor(hot[:, :, :], number, k.idxf[:, :, c:c + 1].broadcast_to(wide), ALU.is_equal))
        step(nc.vector.tensor_tensor(hot[:, :, :], hot[:, :, :], k.w2[:, :, c:c + 1].broadcast_to(wide), ALU.mult))
    step(nc.vector.tensor_tensor(k.comb[:, :, 0:E], k.l[:, :, :], k.hot[:, :, :], ALU.add))
    return cnt[0]


LOGITS_LESS_MAX = 3


def route_scalar(nc, act, k, sem, exped):
    act.wait_ge(sem, LOGITS_LESS_MAX)
    nc.scalar.activation(k.l[:, :, :], k.l[:, :, :], ACT.Exp).then_inc(exped, 1)


def route_buffers(m, at, name, E, n_comb):
    k = Parts()
    k.l = m.sb(name + "_l", [P, NT, E], F32, at)
    k.hot = m.sb(name + "_hot", [P, NT, E], F32, at + 512)
    k.top = m.sb(name + "_top", [P, NT, 8], F32, at + 1024)
    k.idx = m.sb(name + "_idx", [P, NT, 8], U32, at + 1536)
    k.idxf = m.sb(name + "_idxf", [P, NT, 2], F32, at + 2048)
    k.w2 = m.sb(name + "_w2", [P, NT, 2], F32, at + 2176)
    k.mx = m.sb(name + "_mx", [P, NT], F32, at + 2304)
    k.iota = m.sb(name + "_iota", [P, 8], F32, at + 2368)
    k.comb = m.sb(name + "_comb", [P, NT, n_comb], F32, at + 2400)
    return k


ROUTE_BYTES = 2400 + NT * 10 * 4


def stage_moe0(nc, m, d):
    E, EA = 8, 10
    HM = 128
    at = m.R
    k = route_buffers(m, at, "moe0", E, EA)
    at += ROUTE_BYTES
    wt = m.sb("moe0_wt", [P, DC, E], F32, at)
    wg = m.sb("moe0_wg", [64, E], F32, at + 64)
    g = m.sb("moe0_g", [64, B], F32, at + 96)
    gb = m.sb("moe0_gb", [64, B, P], F32, at + 128)
    at += 128 + B * P * 4
    w_gate = [m.sb(f"moe0_gate{i}", [P, DC, HM], F32, at + i * 3072) for i in range(2)]
    w_up = [m.sb(f"moe0_up{i}", [P, DC, HM], F32, at + i * 3072 + 1024) for i in range(2)]
    w_down = [m.sb(f"moe0_down{i}", [P, D], F32, at + i * 3072 + 2048) for i in range(2)]
    at += 2 * 3072
    leak = [m.sb(f"moe0_leak{i}", [P, GRP], F32, at + i * 4096) for i in range(2)]
    gate = [m.sb(f"moe0_act{i}", [P, GRP], F32, at + i * 4096 + 2048) for i in range(2)]
    at += 2 * 4096
    hid = [m.sb(f"moe0_hid{i}", [P, GRP], F32, at + i * 2048) for i in range(2)]

    small, weights = m.sem("moe0_small_loaded"), [m.sem(f"moe0_weights_loaded{i}") for i in range(2)]
    turned, freed = m.sem("moe0_turned"), m.sem("moe0_freed")
    g_wide, logits, steps, exped, made = (m.sem("moe0_" + s) for s in
                                          ("g_wide", "logits", "steps", "exped", "made"))

    def load(sp, e, i):
        sp.dma_start(w_gate[i][:, :, :], d["moe0_gate"][bass.ds(e, 1)].rearrange("e (c p) m -> p (e c) m", p=P)).then_inc(weights[i], 16)
        sp.dma_start(w_up[i][:, :, :], d["moe0_up"][bass.ds(e, 1)].rearrange("e (c p) m -> p (e c) m", p=P)).then_inc(weights[i], 16)
        sp.dma_start(w_down[i][:, :], d["moe0_down"][bass.ds(e, 1)].rearrange("e m d -> (e m) d")).then_inc(weights[i], 16)

    with nc.Block() as block:
        @block.sync
        def _(sp):
            sp.dma_start(wt[:, :, :], d["L0_cond_wt_t"].rearrange("(c p) e -> p c e", p=P)).then_inc(small, 16)
            sp.dma_start(wg[:, :], d["L0_cond_wg_t"]).then_inc(small, 16)
            sp.dma_start(g[:, :], d["cond_t"]).then_inc(small, 16)
            for i in range(2):
                load(sp, i, i)

        @block.gpsimd
        def _(pool):
            nc.gpsimd.iota(k.iota[:, :], pattern=[[1, 8]], base=0, channel_multiplier=0,
                           allow_small_or_imprecise_dtypes=True).then_inc(made, 1)
            nc.gpsimd.memset(k.comb[:, :, E:EA], 1.0).then_inc(made, 1)

        @block.tensor
        def _(pe):
            turn_tensor(nc, pe, m, m.X, turned, freed)
            pe.wait_ge(freed, DC * NG)
            pe.wait_ge(small, 48)
            pe.wait_ge(g_wide, 1)
            for t in range(NT):
                out = m.O[0][:, t * E:(t + 1) * E]
                for c in range(DC):
                    nc.tensor.matmul(out, m.XT[:, c, t * P:(t + 1) * P], wt[:, c, :], start=(c == 0), stop=False)
                last = nc.tensor.matmul(out, gb[:, t // QB, :], wg[:, :], start=False, stop=True)
            last.then_inc(logits, 1)

        @block.scalar
        def _(act):
            turn_scalar(nc, act, m, m.XT, turned, freed)
            route_scalar(nc, act, k, steps, exped)

        @block.vector
        def _(dve):
            dve.wait_ge(small, 48)
            nc.vector.tensor_copy(gb[:, :, :], g[:, :].unsqueeze(2).broadcast_to([64, B, P])).then_inc(g_wide, 1)
            nc.vector.memset(m.Y[:, :, :], 0.0)
            dve.wait_ge(made, 2)
            dve.wait_ge(logits, 1)
            route_vector(nc, dve, m, k, m.O[0][:, 0:NT * E].rearrange("p (t e) -> p t e", e=E), 0.5, 1e-20, E,
                         steps, exped)

    up, leaked, gated, hidden, down, added = (m.sem("moe0_" + s) for s in
                                              ("up", "leaked", "gated", "hidden", "down", "added"))
    JOBS = 2 * NG
    TILES = 2 * NT
    with nc.Block() as block:
        @block.sync
        def _(sp):
            with sp.Fori(0, EA // 2 - 1) as it:
                for i in range(2):
                    sp.wait_ge(down, it * TILES + (i + 1) * NT)
                    load(sp, 2 * it + 2 + i, i)

        @block.tensor
        def _(pe):
            def project_up(it, j):
                i, n = divmod(j, NG)
                if n == 0:
                    pe.wait_ge(weights[i], it * 48 + 48)
                if j >= 2:
                    pe.wait_ge(hidden, it * JOBS + j - 1)
                for w, col in ((w_gate[i], 0), (w_up[i], GRP)):
                    for c in range(DC):
                        last = nc.tensor.matmul(m.S[j % 2][:, col:col + GRP], w[:, c, :],
                                                m.XT[:, c, n * GRP:(n + 1) * GRP], start=(c == 0), stop=(c == DC - 1))
                last.then_inc(up, 1)

            def project_down(it, j):
                i, n = divmod(j, NG)
                pe.wait_ge(hidden, it * JOBS + j + 1)
                for t in range(4):
                    q = 4 * j + t
                    if q >= 4:
                        pe.wait_ge(added, it * TILES + q - 3)
                    nc.tensor.matmul(m.TO[q % 4][:, 0:D], hid[j % 2][:, t * P:(t + 1) * P], w_down[i][:, :],
                                     start=True, stop=True).then_inc(down, 1)

            with pe.Fori(0, EA // 2) as it:
                project_up(it, 0)
                for j in range(1, JOBS):
                    project_up(it, j)
                    project_down(it, j - 1)
                project_down(it, JOBS - 1)
                pe.wait_ge(added, (it + 1) * TILES)

        @block.scalar
        def _(act):
            with act.Fori(0, EA // 2) as it:
                for j in range(JOBS):
                    act.wait_ge(up, it * JOBS + j + 1)
                    if j >= 2:
                        act.wait_ge(gated, it * JOBS + j - 1)
                    nc.scalar.activation(leak[j % 2][:, :], m.S[j % 2][:, 0:GRP], ACT.Copy, scale=0.01).then_inc(leaked, 1)
                act.wait_ge(gated, (it + 1) * JOBS)

        @block.vector
        def _(dve):
            def hidden_of(it, j):
                dve.wait_ge(leaked, it * JOBS + j + 1)
                nc.vector.tensor_tensor(gate[j % 2][:, :], m.S[j % 2][:, 0:GRP], leak[j % 2][:, :], ALU.max).then_inc(gated, 1)
                dve.wait_ge(gated, it * JOBS + j + 1)
                nc.vector.tensor_tensor(hid[j % 2][:, :], gate[j % 2][:, :], m.S[j % 2][:, GRP:2 * GRP], ALU.mult).then_inc(hidden, 1)

            def add_up(it, j):
                i, n = divmod(j, NG)
                for t in range(4):
                    q, tile = 4 * j + t, 4 * n + t
                    dve.wait_ge(down, it * TILES + q + 1)
                    nc.vector.scalar_tensor_tensor(m.Y[:, tile, :], m.TO[q % 4][:, 0:D],
                                                   k.comb[:, tile, bass.ds(2 * it + i, 1)], m.Y[:, tile, :],
                                                   ALU.mult, ALU.add).then_inc(added, 1)

            with dve.Fori(0, EA // 2) as it:
                hidden_of(it, 0)
                for j in range(1, JOBS):
                    if j >= 2:
                        pass
                    hidden_of(it, j)
                    add_up(it, j - 1)
                add_up(it, JOBS - 1)


def plan(units, heads, per_head):
    R = heads * per_head
    steps, chunk = [("row", 0, r) for r in range(R)], 0
    for n, (b, q0) in enumerate(units):
        blocks = q0 + per_head
        rows = list(range(R)) if n + 1 < len(units) else []
        mine = [("null", n)]
        placed = 0
        for kb in range(blocks):
            while placed < len(rows) and placed * blocks < (kb + 1) * len(rows):
                mine.append(("row", n + 1, rows[placed]))
                placed += 1
            mine.append(("chunk", n, kb, chunk))
            chunk += 1
            if kb == 0:
                mine.append(("den", n))
                if n:
                    mine.append(("fin", n - 1))
        steps += mine
    steps.append(("fin", len(units) - 1))
    return steps, chunk


def stage_attention(nc, m, d, a):
    H, PH, U = a.heads, a.per_head, len(a.units)
    R, W = H * PH, P // H
    steps, CH = plan(a.units, H, PH)
    RPI = U * R
    by_act = [c % 5 not in (1, 3) for c in range(CH)]
    seen = {True: 0, False: 0}
    copies = []
    for c in range(CH):
        seen[by_act[c]] += 1
        copies.append(seen[by_act[c]])
    EA, ED = seen[True], seen[False]
    n_ = a.name
    qk, added, exped, turned, by_a, by_d, null_arg, null_exp, den, inv, wide, spread, spread_sb, done, pick, pick_pool = (
        m.sem(f"{n_}_{s}") for s in ("qk", "added", "exped", "turned", "copied_act", "copied_dve", "null_arg",
                                     "null_exp", "den", "inv", "inv_wide", "spread", "spread_sb", "done", "pick", "pick_pool"))
    at = a.at
    Pr = [m.sb(f"{n_}_p{i}", [P, 4, S], F32, at + i * 16384) for i in range(2)]
    PT = [m.sb(f"{n_}_pt{i}", [P, 512], F32, at + 32768 + i * 2048) for i in range(2)]
    at += 32768 + 4096
    RB = [m.sb(f"{n_}_rb{i}", [P, PH, P], F32, at + i * 1024) for i in range(2)]
    RS = m.sb(f"{n_}_rs", [P, PH * P], F32, at + 2048)
    at += 2048 + 1024
    tiny = [m.sb(f"{n_}_{s}{i}", [P, R], F32, at + 64 * q + 32 * i)
            for q, s in enumerate(("negm", "rsum", "nulla", "nulle", "dn", "rinv")) for i in range(2)]
    negm, rsum, nulla, nulle, dn, rinv = (tiny[2 * q:2 * q + 2] for q in range(6))
    at += 6 * 64

    def blk(n, r):
        h, s = divmod(r, PH)
        b, q0 = a.units[n]
        return h, b, q0 + s

    def copied(eng, it, c):
        if by_act[c]:
            eng.wait_ge(by_a, it * EA + copies[c])
        else:
            eng.wait_ge(by_d, it * ED + copies[c])

    def live(n, kb):
        return max(0, kb - a.units[n][1])

    def copy_views(n, kb, c):
        s0 = live(n, kb)
        cut = lambda x: x.rearrange("p (h s q) -> p h s q", s=PH, q=P)[:, :, s0:PH, :]
        return cut(PT[c % 2][:, 0:R * P]), cut(m.T[c % 2][:, 0:R * P])

    with nc.Block() as block:
        if a.sync is not None:
            @block.sync
            def _(sp):
                a.sync(sp, added, RPI)

        @block.gpsimd
        def _(pool):
            with loop(pool, a.iters) as it:
                if a.pool_first is not None:
                    a.pool_first(pool, it)
                for n in range(U):
                    if a.pool_bias is not None and n + 1 < 4:
                        a.pool_bias(pool, it, n + 1)
                    pool.wait_ge(inv, it * U + n + 1)
                    if n >= 2:
                        pool.wait_ge(spread, it * U + n - 1)
                    if a.iters > 1:
                        hold(nc.gpsimd, pick_pool)
                    nc.gpsimd.tensor_copy(RB[n % 2][:, :, :].rearrange("p s (h w) -> p s h w", h=H),
                                          rinv[n % 2][:, :].rearrange("p (h s) -> p s h", s=PH).unsqueeze(3)
                                          .broadcast_to([P, PH, H, W])).then_inc(wide, 1)
                pool.wait_ge(done, (it + 1) * U)
                if a.iters > 1:
                    hold(nc.gpsimd, pick_pool)

        @block.tensor
        def _(pe):
            def attend(it, n, kb, c):
                b, q0 = a.units[n]
                copied(pe, it, c)
                if kb == 0 and n >= 2:
                    pe.wait_ge(done, it * U + n - 1)
                s0 = live(n, kb)
                for h in range(H):
                    last = nc.tensor.matmul(m.O[n % 2][h * W:(h + 1) * W, s0 * P:PH * P], a.values(h, b, kb),
                                            PT[c % 2][:, (h * PH + s0) * P:(h + 1) * PH * P],
                                            start=(kb == 0), stop=(kb == q0 + PH - 1))
                if kb == q0 + PH - 1:
                    pe.wait_ge(wide, it * U + n + 1)
                    for s in range(PH):
                        last = nc.tensor.matmul(m.O[n % 2][:, 256 + s * P:256 + (s + 1) * P], RB[n % 2][:, s, :],
                                                m.ident[:, :], start=True, stop=True)
                    last.then_inc(spread, 1)

            with loop(pe, a.iters) as it:
                a.tensor_first(pe, it)
                before = None
                for step in steps:
                    if step[0] == "row":
                        _, n, r = step
                        h, b, q = blk(n, r)
                        x = n * R + r
                        if x >= 2:
                            pe.wait_ge(added, it * RPI + x - 1)
                        L = (q + 1) * P
                        for lo in range(0, L, 512):
                            hi = min(lo + 512, L)
                            last = nc.tensor.matmul(m.S[x % 2][:, lo:hi], a.scores(h, b, q), a.keys(h, b, lo, hi),
                                                    start=True, stop=True)
                        last.then_inc(qk, 1)
                    elif step[0] == "chunk":
                        _, n, kb, c = step
                        if kb == 0:
                            pe.wait_ge(exped, it * RPI + (n + 1) * R)
                        if c >= 2:
                            copied(pe, it, c - 2)
                        for r in range(R):
                            if blk(n, r)[2] >= kb:
                                last = nc.tensor.transpose(m.T[c % 2][:, r * P:(r + 1) * P],
                                                           Pr[n % 2][:, r, kb * P:(kb + 1) * P], m.ident[:, :])
                        last.then_inc(turned, 1)
                        if before is not None:
                            attend(it, *before)
                        before = (n, kb, c)
                attend(it, *before)
                pe.wait_ge(done, (it + 1) * U)

        @block.scalar
        def _(act):
            with loop(act, a.iters) as it:
                a.scalar_first(act, it)
                for step in steps:
                    if step[0] == "row":
                        _, n, r = step
                        L = (blk(n, r)[2] + 1) * P
                        act.wait_ge(added, it * RPI + n * R + r + 1)
                        p = Pr[n % 2][:, r, 0:L]
                        nc.scalar.activation(p, p, ACT.Exp, bias=negm[n % 2][:, r:r + 1], scale=-1.0,
                                             accum_out=rsum[n % 2][:, r:r + 1]).then_inc(exped, 1)
                    elif step[0] == "chunk" and by_act[step[3]]:
                        _, n, kb, c = step
                        act.wait_ge(turned, it * CH + c + 1)
                        o, i = copy_views(n, kb, c)
                        nc.scalar.copy(o, i).then_inc(by_a, 1)
                    elif step[0] == "null" and a.null:
                        n = step[1]
                        act.wait_ge(null_arg, it * U + n + 1)
                        nc.scalar.activation(nulle[n % 2][:, :], nulla[n % 2][:, :], ACT.Exp).then_inc(null_exp, 1)
                    elif step[0] == "fin":
                        n = step[1]
                        act.wait_ge(spread, it * U + n + 1)
                        if n >= 1:
                            act.wait_ge(done, it * U + n)
                        nc.scalar.copy(RS[:, :], m.O[n % 2][:, 256:256 + PH * P]).then_inc(spread_sb, 1)

        @block.vector
        def _(dve):
            with loop(dve, a.iters) as it:
                a.vector_first(dve, it)
                for step in steps:
                    if step[0] == "row":
                        _, n, r = step
                        h, b, q = blk(n, r)
                        L = (q + 1) * P
                        if a.bias_ready is not None:
                            a.bias_ready(dve, it, n, r)
                        dve.wait_ge(qk, it * RPI + n * R + r + 1)
                        if a.iters > 1:
                            hold(nc.vector, pick)
                        nc.vector.tensor_tensor_reduce(
                            out=Pr[n % 2][:, r, 0:L], in0=m.S[(n * R + r) % 2][:, 0:L], in1=a.bias(h, b, q, L),
                            scale=-1.0, scalar=a.null_score(h, b, q) if a.null else 3.0e38, op0=ALU.add, op1=ALU.min,
                            accum_out=negm[n % 2][:, r:r + 1]).then_inc(added, 1)
                    elif step[0] == "chunk" and not by_act[step[3]]:
                        _, n, kb, c = step
                        dve.wait_ge(turned, it * CH + c + 1)
                        o, i = copy_views(n, kb, c)
                        nc.vector.tensor_copy(o, i).then_inc(by_d, 1)
                    elif step[0] == "null" and a.null:
                        n = step[1]
                        dve.wait_ge(added, it * RPI + (n + 1) * R)
                        nc.vector.tensor_tensor(nulla[n % 2][:, :].rearrange("p (h s) -> p h s", s=PH),
                                                negm[n % 2][:, :].rearrange("p (h s) -> p h s", s=PH),
                                                a.null_scores(*a.units[n]), ALU.subtract).then_inc(null_arg, 1)
                    elif step[0] == "den":
                        n = step[1]
                        total = rsum[n % 2]
                        dve.wait_ge(exped, it * RPI + (n + 1) * R)
                        if a.null:
                            dve.wait_ge(null_exp, it * U + n + 1)
                            nc.vector.tensor_tensor(dn[n % 2][:, :], rsum[n % 2][:, :], nulle[n % 2][:, :],
                                                    ALU.add).then_inc(den, 1)
                            dve.wait_ge(den, it * U + n + 1)
                            total = dn[n % 2]
                        if n >= 2:
                            dve.wait_ge(wide, it * U + n - 1)
                        nc.vector.reciprocal(rinv[n % 2][:, :], total[:, :]).then_inc(inv, 1)
                    elif step[0] == "fin":
                        n = step[1]
                        b, q0 = a.units[n]
                        dve.wait_ge(spread_sb, it * U + n + 1)
                        nc.vector.tensor_tensor(a.output(it, b, q0), m.O[n % 2][:, 0:PH * P], RS[:, :],
                                                ALU.mult).then_inc(done, 1)


def stage_project_out(nc, m, name, n_chunks, w_out, w_dram, row, out):
    loaded, ready, taken = m.sem(name + "_loaded"), m.sem(name + "_ready"), m.sem(name + "_taken")
    rowed, rowed_sb = m.sem(name + "_row"), m.sem(name + "_row_sb")
    with nc.Block() as block:
        @block.sync
        def _(sp):
            sp.dma_start(w_out[:, :, :], w_dram.rearrange("(c p) d -> p c d", p=P)).then_inc(loaded, 16)

        @block.tensor
        def _(pe):
            pe.wait_ge(loaded, 16)
            if row is not None:
                for c in range(n_chunks):
                    last = nc.tensor.matmul(m.O[0][:, 0:D], row.nv_wide[:, :], w_out[:, c, :],
                                            start=(c == 0), stop=(c == n_chunks - 1))
                last.then_inc(rowed, 1)
            for t in range(NT):
                if t >= 4:
                    pe.wait_ge(taken, t - 3)
                for c in range(n_chunks):
                    last = nc.tensor.matmul(m.SH[t % 4][:, 0:D], m.OT[:, c, t * P:(t + 1) * P], w_out[:, c, :],
                                            start=(c == 0), stop=(c == n_chunks - 1))
                last.then_inc(ready, 1)

        @block.vector
        def _(dve):
            if row is not None:
                dve.wait_ge(rowed, 1)
                nc.vector.tensor_copy(row.out[:, :], m.O[0][:, 0:D]).then_inc(rowed_sb, 1)
                dve.wait_ge(rowed_sb, 1)
            for t in range(NT):
                dve.wait_ge(ready, t + 1)
                nc.vector.tensor_tensor(out[:, t, :], m.SH[t % 4][:, 0:D],
                                        row.out[:, :] if row is not None else out[:, t, :], ALU.add).then_inc(taken, 1)


def causal_units(per_head):
    return [(b, q0) for b in range(B) for q0 in range(0, QB, per_head)]


def stage_attn0(nc, m, d):
    H, G, HD, W = 16, 4, 16, 32
    IT = H // G
    at = m.R + 65536
    QT = m.sb("attn0_qt", [P, B * S], F32, at)
    KT = m.sb("attn0_kt", [P, B * S], F32, at + 8192)
    VA = m.sb("attn0_va", [P, NT, H * W], F32, at + 16384)
    VG = m.sb("attn0_vg", [P, NT, P], F32, m.YAT)
    causal = m.sb("attn0_causal", [P, S], F32, m.YAT + 8192)
    wv = m.sb("attn0_wv", [P, DC, H * W], F32, m.YAT + 12288)
    wq = m.sb("attn0_wq", [P, DC, P], F32, at + 49152)
    wk = m.sb("attn0_wk", [P, DC, P], F32, at + 50176)
    at += 51200

    loaded, w_loaded = m.sem("attn0_wv_loaded"), m.sem("attn0_w_loaded")
    valued, taken, made = m.sem("attn0_valued"), m.sem("attn0_taken"), m.sem("attn0_made")

    def load(sp, g):
        cols = lambda w: w[:, bass.ds(g * P, P)].rearrange("(c p) n -> p c n", p=P)
        sp.dma_start(wq[:, :, :], cols(d["attn0_wq"])).then_inc(w_loaded, 16)
        sp.dma_start(wk[:, :, :], cols(d["attn0_wk"])).then_inc(w_loaded, 16)

    stage_turn(nc, m, "attn0_in", m.Y, m.XT)
    with nc.Block() as block:
        @block.sync
        def _(sp):
            sp.dma_start(wv[:, :, :], d["attn0_wv"].rearrange("(c p) n -> p c n", p=P)).then_inc(loaded, 16)
            load(sp, 0)

        @block.gpsimd
        def _(pool):
            nc.gpsimd.memset(causal[:, :], 0.0).then_inc(made, 1)
            pool.wait_ge(made, 1)
            nc.gpsimd.affine_select(out=causal[:, :], in_=causal[:, :], compare_op=ALU.is_ge, fill=FAR,
                                    base=S - P, pattern=[[-1, S]], channel_multiplier=1).then_inc(made, 1)

        @block.tensor
        def _(pe):
            pe.wait_ge(loaded, 16)
            for t in range(NT):
                if t >= 4:
                    pe.wait_ge(taken, t - 3)
                for c in range(DC):
                    last = nc.tensor.matmul(m.SH[t % 4][:, :], m.XT[:, c, t * P:(t + 1) * P], wv[:, c, :],
                                            start=(c == 0), stop=(c == DC - 1))
                last.then_inc(valued, 1)

        @block.vector
        def _(dve):
            for t in range(NT):
                dve.wait_ge(valued, t + 1)
                nc.vector.tensor_copy(VA[:, t, :], m.SH[t % 4][:, :]).then_inc(taken, 1)

    projected, q_taken, k_taken, v_ready = (m.sem("attn0_" + s) for s in ("projected", "q_taken", "k_taken", "v_ready"))

    def sync(sp, added, rpi):
        with sp.Fori(0, IT - 1) as it:
            sp.wait_ge(projected, it * 8 + 8)
            load(sp, it + 1)

    def pool_first(pool, it):
        if IT > 1:
            nc.gpsimd.tensor_copy(VG[:, :, :], VA[:, :, bass.ds(it * P, P)]).then_inc(v_ready, 1)

    def tensor_first(pe, it):
        pe.wait_ge(w_loaded, it * 32 + 32)
        for j in range(8):
            g, w, taken_ = j // 2, (wq, wk)[j % 2], (q_taken, k_taken)[j % 2]
            if j >= 4:
                pe.wait_ge(taken_, it * 4 + j // 2 - 1)
            for c in range(DC):
                last = nc.tensor.matmul(m.SH[j % 4][:, :], w[:, c, :], m.XT[:, c, g * GRP:(g + 1) * GRP],
                                        start=(c == 0), stop=(c == DC - 1))
            last.then_inc(projected, 1)
        pe.wait_ge(q_taken, it * 4 + 4)
        pe.wait_ge(k_taken, it * 4 + 4)
        pe.wait_ge(v_ready, it + 1)

    def scalar_first(act, it):
        for g in range(4):
            act.wait_ge(projected, it * 8 + 2 * g + 1)
            nc.scalar.mul(QT[:, g * GRP:(g + 1) * GRP], m.SH[(2 * g) % 4][:, :], HD ** -0.5).then_inc(q_taken, 1)

    def vector_first(dve, it):
        for g in range(4):
            dve.wait_ge(projected, it * 8 + 2 * g + 2)
            nc.vector.tensor_copy(KT[:, g * GRP:(g + 1) * GRP], m.SH[(2 * g + 1) % 4][:, :]).then_inc(k_taken, 1)

    a = Parts()
    a.name = "attn0"
    a.iters = IT
    a.heads = G
    a.per_head = 1
    a.units = causal_units(1)
    a.null = False
    a.at = at
    a.sync = sync
    a.pool_first = pool_first
    a.pool_bias = None
    a.bias_ready = None
    a.tensor_first = tensor_first
    a.scalar_first = scalar_first
    a.vector_first = vector_first
    a.scores = lambda h, b, q: QT[h * W:(h + 1) * W, b * S + q * P:b * S + (q + 1) * P]
    a.keys = lambda h, b, lo, hi: KT[h * W:(h + 1) * W, b * S + lo:b * S + hi]
    a.values = lambda h, b, kb: VG[:, b * QB + kb, h * W:(h + 1) * W]
    a.bias = lambda h, b, q, L: causal[:, S - L:S]
    a.output = lambda it, b, q0: m.OT[:, bass.ds(it, 1) if IT > 1 else slice(0, 1), b * S + q0 * P:b * S + (q0 + 1) * P]
    stage_attention(nc, m, d, a)
    w_out = m.sb("attn0_wo", [P, IT, D], F32, m.R + 65536)
    stage_project_out(nc, m, "attn0_out", IT, w_out, d["attn0_wo"], None, m.X)


HEADS, HD = 16, 64
PAIRS = HEADS // 2
SIDE_AT = [sum((q + 1) * P for q in range(qb)) for qb in range(QB + 1)]


def stage_mqa(nc, m, d, name, w, cosine):
    at = m.R + 65536
    QT = m.sb(name + "_qt", [P, 2, B * S], F32, at)
    bias_at = at + 16384
    loop_at = bias_at + 36864
    small = loop_at + 40320
    KT = m.sb(name + "_kt", [P, B * S], F32, m.YAT)
    V = m.sb(name + "_v", [P, NT, HD], F32, m.YAT + 8192)
    wq = m.sb(name + "_wq", [P, DC, P], F32, small)
    g_out = m.sb(name + "_g_out", [P, D], F32, small + 1024)
    nv_wide = m.sb(name + "_nv_wide", [P, P], F32, small + 2048)
    nv_row = m.sb(name + "_nv_row", [P, HD], F32, small + 2560)
    NB = m.sb(name + "_null_bias", [P, HEADS], F32, small + 2816)
    SN = m.sb(name + "_null_score", [P, 2, NT], F32, small + 2880)
    nk = m.sb(name + "_nk", [HD, 8], F32, small + 3008)
    nv = m.sb(name + "_nv", [P, 8], F32, small + 3040)
    qs = m.sb(name + "_qs", [P, 8], F32, small + 3072)
    ks = m.sb(name + "_ks", [HD, 8], F32, small + 3104)
    g_in = m.sb(name + "_g_in", [P, D], F32, loop_at)
    wkv = m.sb(name + "_wkv", [P, DC, 2 * HD], F32, loop_at + 1024)
    mask = m.sb(name + "_mask", [P, B * S], U8, loop_at + 2048)

    loaded, wq_loaded = m.sem(name + "_loaded"), m.sem(name + "_wq_loaded")

    def load_wq(sp, pair):
        sp.dma_start(wq[:, :, :], w.wq[:, bass.ds(pair * P, P)].rearrange("(c p) n -> p c n", p=P)).then_inc(wq_loaded, 16)

    side_loaded = [m.sem(f"{name}_side_loaded{g}") for g in range(4)]
    side = None
    if not cosine:
        side = [m.sb(f"{name}_side{h}", [P, SIDE_AT[QB]], F32, bias_at + h * 18432) for h in range(2)]

    def load_side(sp, pair, g):
        for h in range(2):
            for q in (2 * g, 2 * g + 1):
                sp.dma_start(side[h][:, SIDE_AT[q]:SIDE_AT[q + 1]],
                             d["fside_16xSxS_0"][bass.ds(2 * pair + h, 1), q * P:(q + 1) * P, 0:(q + 1) * P]
                             .rearrange("a q k -> (a q) k")).then_inc(side_loaded[g], 16)

    with nc.Block() as block:
        @block.sync
        def _(sp):
            n_loads = [0]

            def load(dst, src):
                n_loads[0] += 16
                sp.dma_start(dst, src).then_inc(loaded, 16)

            row = lambda v: v.rearrange("(a n) -> a n", a=1)
            column = lambda v: v.rearrange("(n a) -> n a", a=1)
            load(g_in[:, :], row(w.g_in).broadcast_to([P, D]))
            load(g_out[:, :], row(w.g_out).broadcast_to([P, D]))
            load(wkv[:, :, :], w.wkv.rearrange("(c p) n -> p c n", p=P))
            load(NB[:, :], row(w.null_bias).broadcast_to([P, HEADS]))
            load(nk[:, 0:1], column(d["cond_64"].rearrange("a n -> (a n)")[0:HD]))
            for h in range(2):
                load(nv[h * HD:(h + 1) * HD, 0:1], column(d["cond_64"].rearrange("a n -> (a n)")[HD:2 * HD]))
            load(nv_row[:, :], d["cond_64"][1:2, :].broadcast_to([P, HD]))
            load(mask[HD:HD + 1, :], w.mask.rearrange("b s -> (b s)").rearrange("(a n) -> a n", a=1))
            if cosine:
                for h in range(2):
                    load(qs[h * HD:(h + 1) * HD, 0:1], column(w.q_scale))
                load(ks[:, 0:1], column(w.k_scale))
            load_wq(sp, 0)
            if not cosine:
                for g in range(4):
                    load_side(sp, 0, g)
            sp.wait_ge(loaded, n_loads[0])

    stage_norm_turn(nc, m, name + "_in", m.X, m.Y, m.XT, g_in, (loaded, 16), loop_at + 4096)

    sq = [m.sb(f"{name}_sq{i}", [P, GRP], F32, bias_at + 8192 + i * 2048) for i in range(2)] if cosine else None
    nr = [m.sb(f"{name}_nr{i}", [P, GRP], F32, bias_at + 12288 + i * 2048) for i in range(2)] if cosine else None
    rn = [m.sb(f"{name}_rn{i}", [P, GRP], F32, bias_at + 16384 + i * 2048) for i in range(2)] if cosine else None
    halves = m.sb(name + "_halves", [P, P], F32, bias_at + 20480) if cosine else None
    keyed, k_taken, valued, v_taken, steps, made, squared, summed, rooted = (
        m.sem(f"{name}_{s}") for s in ("keyed", "k_taken", "valued", "v_taken", "kv_steps", "made", "squared",
                                       "summed", "rooted"))
    K_PIECES = NG + 1
    with nc.Block() as block:
        @block.tensor
        def _(pe):
            for g in range(NG):
                for c in range(DC):
                    last = nc.tensor.matmul(m.SH[g][0:HD, :], wkv[:, c, 0:HD], m.XT[:, c, g * GRP:(g + 1) * GRP],
                                            start=(c == 0), stop=(c == DC - 1))
                last.then_inc(keyed, 1)
            for t in range(NT):
                if t >= 2:
                    pe.wait_ge(v_taken, t - 1)
                for c in range(DC):
                    last = nc.tensor.matmul(m.O[t % 2][:, 0:HD], m.XT[:, c, t * P:(t + 1) * P], wkv[:, c, HD:2 * HD],
                                            start=(c == 0), stop=(c == DC - 1))
                last.then_inc(valued, 1)
            if cosine:
                pe.wait_ge(made, 3)
                for g in range(K_PIECES):
                    n = GRP if g < NG else 1
                    pe.wait_ge(squared, g + 1)
                    if g >= 2:
                        pe.wait_ge(rooted, g - 1)
                    nc.tensor.matmul(m.T[g % 2][0:HD, 0:n], halves[0:HD, 0:HD], sq[g % 2][0:HD, 0:n],
                                     start=True, stop=True).then_inc(summed, 1)

        @block.scalar
        def _(act):
            for g in range(NG):
                act.wait_ge(keyed, g + 1)
                nc.scalar.copy(KT[0:HD, g * GRP:(g + 1) * GRP], m.SH[g][0:HD, :]).then_inc(k_taken, 1)
            if cosine:
                for g in range(K_PIECES):
                    n = GRP if g < NG else 1
                    if g < NG:
                        act.wait_ge(k_taken, g + 1)
                    if g >= 2:
                        act.wait_ge(summed, g - 1)
                    src = KT[0:HD, g * GRP:(g + 1) * GRP] if g < NG else nk[:, 0:1]
                    nc.scalar.activation(sq[g % 2][0:HD, 0:n], src, ACT.Square).then_inc(squared, 1)
                    act.wait_ge(summed, g + 1)
                    if g >= 2:
                        act.wait_ge(steps, 3 * (g - 1))
                    nc.scalar.activation(nr[g % 2][0:HD, 0:n], m.T[g % 2][0:HD, 0:n], ACT.Sqrt).then_inc(rooted, 1)

        @block.gpsimd
        def _(pool):
            nc.gpsimd.memset(QT[HD:HD + 1, :, :], 1.0).then_inc(made, 1)
            if cosine:
                pool.wait_ge(made, 1)
                nc.gpsimd.memset(halves[:, :], 0.0).then_inc(made, 1)
                pool.wait_ge(made, 2)
                nc.gpsimd.memset(halves[0:HD, 0:HD], 1.0)
                nc.gpsimd.memset(halves[HD:P, HD:P], 1.0).then_inc(made, 1)

        @block.vector
        def _(dve):
            nc.vector.tensor_scalar(KT[HD:HD + 1, :], mask[HD:HD + 1, :], 1.0e30, -1.0e30, ALU.mult, ALU.add)
            nc.vector.tensor_copy(nv_wide[:, :], nv[:, 0:1].broadcast_to([P, P]))
            for t in range(NT):
                dve.wait_ge(valued, t + 1)
                nc.vector.tensor_tensor(V[:, t, :], m.O[t % 2][:, 0:HD], nv_row[:, :], ALU.subtract).then_inc(v_taken, 1)
            if cosine:
                for g in range(K_PIECES):
                    n = GRP if g < NG else 1
                    dve.wait_ge(rooted, g + 1)
                    nc.vector.tensor_scalar(nr[g % 2][0:HD, 0:n], nr[g % 2][0:HD, 0:n], 1e-12, None, ALU.max).then_inc(steps, 1)
                    dve.wait_ge(steps, 3 * g + 1)
                    nc.vector.reciprocal(rn[g % 2][0:HD, 0:n], nr[g % 2][0:HD, 0:n]).then_inc(steps, 1)
                    dve.wait_ge(steps, 3 * g + 2)
                    piece = KT[0:HD, g * GRP:(g + 1) * GRP] if g < NG else nk[:, 0:1]
                    nc.vector.scalar_tensor_tensor(piece, piece, ks[:, 0:1], rn[g % 2][0:HD, 0:n],
                                                   ALU.mult, ALU.mult).then_inc(steps, 1)
                nc.vector.tensor_scalar(qs[:, 1:2], qs[:, 0:1], 8.0, None, ALU.mult)

    toep = [m.sb(f"{name}_toep{h}", [P, S], F32, bias_at + h * 4096) for h in range(2)] if cosine else None
    toep_loaded, side_masked = m.sem(name + "_toep_loaded"), [m.sem(f"{name}_side_masked{g}") for g in range(4)]
    projected, q0_taken, q1_taken, nulled, null_taken, q_sq, q_sum, q_root, q_steps, pick = (
        m.sem(f"{name}_{s}") for s in ("projected", "q0_taken", "q1_taken", "nulled", "null_taken", "q_squared",
                                       "q_summed", "q_rooted", "q_steps", "side_pick"))
    units = causal_units(2)

    def load_toep(sp, pair):
        for h in range(2):
            far = d["distance"][bass.ds(2 * pair + h, 1), 1:1 + S]
            src = bass.AP(far.tensor, far.offset, [[1, P], [1, S]])
            sp.dma_start(toep[h][:, :], src).then_inc(toep_loaded, 16)

    def sync(sp, added, rpi):
        if cosine:
            load_toep(sp, 0)
        with sp.Fori(0, PAIRS - 1) as it:
            sp.wait_ge(projected, it * NG + NG)
            load_wq(sp, it + 1)
            if cosine:
                sp.wait_ge(added, (it + 1) * rpi)
                load_toep(sp, it + 1)
            else:
                for g in range(4):
                    sp.wait_ge(added, it * rpi + 4 * (4 + g + 1))
                    load_side(sp, it + 1, g)

    def toep_back(h, L):
        cols = toep[h][:, 0:L]
        return bass.AP(cols.tensor, cols.offset + L - 1, [cols.ap[0], [-1, L]])

    def pool_bias(pool, it, g):
        pool.wait_ge(side_loaded[g], (it + 1) * 64)
        hold(nc.gpsimd, pick)
        for h in range(2):
            for q in (2 * g, 2 * g + 1):
                block_ = side[h][:, SIDE_AT[q + 1] - P:SIDE_AT[q + 1]]
                last = nc.gpsimd.affine_select(out=block_, in_=block_, compare_op=ALU.is_ge, fill=FAR, base=0,
                                               pattern=[[-1, P]], channel_multiplier=1)
        last.then_inc(side_masked[g], 1)

    def bias_ready(dve, it, n, r):
        if cosine and n == 0 and r == 0:
            dve.wait_ge(toep_loaded, (it + 1) * 32)
        if not cosine and n < 4 and r == 0:
            dve.wait_ge(side_masked[n], it + 1)

    def tensor_first(pe, it):
        pe.wait_ge(wq_loaded, it * 16 + 16)
        for g in range(NG):
            for c in range(DC):
                last = nc.tensor.matmul(m.SH[g][:, :], wq[:, c, :], m.XT[:, c, g * GRP:(g + 1) * GRP],
                                        start=(c == 0), stop=(c == DC - 1))
            last.then_inc(projected, 1)
        if cosine:
            for g in range(NG):
                pe.wait_ge(q_sq, it * NG + g + 1)
                if g >= 2:
                    pe.wait_ge(q_root, it * NG + g - 1)
                nc.tensor.matmul(m.T[g % 2][:, :], halves[:, :], sq[g % 2][:, :], start=True, stop=True).then_inc(q_sum, 1)
        pe.wait_ge(q0_taken, it * NG + NG)
        pe.wait_ge(q1_taken, it * NG + NG)
        for h in range(2):
            for t in range(NT):
                last = nc.tensor.matmul(m.O[0][:, h * NT + t:h * NT + t + 1], QT[0:HD, h, t * P:(t + 1) * P], nk[:, 0:1],
                                        start=True, stop=True)
        last.then_inc(nulled, 1)
        pe.wait_ge(null_taken, it + 1)

    def scalar_first(act, it):
        if cosine:
            for g in range(NG):
                act.wait_ge(projected, it * NG + g + 1)
                if g >= 2:
                    act.wait_ge(q_sum, it * NG + g - 1)
                nc.scalar.activation(sq[g % 2][:, :], m.SH[g][:, :], ACT.Square).then_inc(q_sq, 1)
            for g in range(NG):
                act.wait_ge(q_sum, it * NG + g + 1)
                if g >= 2:
                    act.wait_ge(q1_taken, it * NG + g - 1)
                nc.scalar.activation(nr[g % 2][:, :], m.T[g % 2][:, :], ACT.Sqrt).then_inc(q_root, 1)
        else:
            for g in range(NG):
                act.wait_ge(projected, it * NG + g + 1)
                nc.scalar.mul(QT[0:HD, 0, g * GRP:(g + 1) * GRP], m.SH[g][0:HD, :], HD ** -0.5).then_inc(q0_taken, 1)

    def vector_first(dve, it):
        for g in range(NG):
            cols = slice(g * GRP, (g + 1) * GRP)
            if cosine:
                dve.wait_ge(q_root, it * NG + g + 1)
                nc.vector.tensor_scalar(nr[g % 2][:, :], nr[g % 2][:, :], 1e-12, None, ALU.max).then_inc(q_steps, 1)
                dve.wait_ge(q_steps, it * 2 * NG + 2 * g + 1)
                nc.vector.reciprocal(rn[g % 2][:, :], nr[g % 2][:, :]).then_inc(q_steps, 1)
                dve.wait_ge(q_steps, it * 2 * NG + 2 * g + 2)
                for h, taken in ((0, q0_taken), (1, q1_taken)):
                    half = slice(h * HD, (h + 1) * HD)
                    nc.vector.scalar_tensor_tensor(QT[0:HD, h, cols], m.SH[g][half, :], qs[half, 1:2], rn[g % 2][half, :],
                                                   ALU.mult, ALU.mult).then_inc(taken, 1)
            else:
                dve.wait_ge(projected, it * NG + g + 1)
                nc.vector.tensor_scalar(QT[0:HD, 1, cols], m.SH[g][HD:P, :], HD ** -0.5, None, ALU.mult).then_inc(q1_taken, 1)
        dve.wait_ge(nulled, it + 1)
        nc.vector.scalar_tensor_tensor(SN[:, :, :], m.O[0][:, 0:2 * NT].rearrange("p (h t) -> p h t", h=2), -1.0,
                                       NB[:, bass.ds(2 * it, 2)].unsqueeze(2).broadcast_to([P, 2, NT]),
                                       ALU.mult, ALU.subtract).then_inc(null_taken, 1)
        dve.wait_ge(null_taken, it + 1)

    a = Parts()
    a.name = name
    a.iters = PAIRS
    a.heads = 2
    a.per_head = 2
    a.units = units
    a.null = True
    a.at = loop_at
    a.sync = sync
    a.pool_first = None if cosine else (lambda pool, it: pool_bias(pool, it, 0))
    a.pool_bias = None if cosine else pool_bias
    a.bias_ready = bias_ready
    a.tensor_first = tensor_first
    a.scalar_first = scalar_first
    a.vector_first = vector_first
    a.scores = lambda h, b, q: QT[0:HD + 1, h, b * S + q * P:b * S + (q + 1) * P]
    a.keys = lambda h, b, lo, hi: KT[0:HD + 1, b * S + lo:b * S + hi]
    a.values = lambda h, b, kb: V[:, b * QB + kb, :]
    a.bias = lambda h, b, q, L: toep_back(h, L) if cosine else side[h][:, SIDE_AT[q]:SIDE_AT[q + 1]]
    a.null_score = lambda h, b, q: SN[:, h, b * QB + q:b * QB + q + 1]
    a.null_scores = lambda b, q0: SN[:, :, b * QB + q0:b * QB + q0 + 2]
    a.output = lambda it, b, q0: m.OT[:, bass.ds(it, 1), b * S + q0 * P:b * S + (q0 + 2) * P]
    stage_attention(nc, m, d, a)
    w_out = m.sb(name + "_wo", [P, PAIRS, D], F32, loop_at)
    row = Parts()
    row.nv_wide = nv_wide
    row.out = m.sb(name + "_null_row", [P, D], F32, loop_at + 8192)
    stage_project_out(nc, m, name + "_out", PAIRS, w_out, w.wo, row, m.Y)
    stage_norm_turn(nc, m, name + "_post", m.Y, m.Y, None, g_out, (loaded, 32), loop_at + 16384)


def stage_cond2_0(nc, m, d):
    w = Parts()
    w.wq = d["L0_cond2_Wq"]
    w.wkv = d["L0_cond2_Wkv"]
    w.wo = d["L0_cond2_Wo"]
    w.g_in = d["L0_cond2_g_in"]
    w.g_out = d["L0_cond2_g_out"]
    w.null_bias = d["L0_cond2_null_attn_bias"]
    w.mask = d["mask_bk0"]
    stage_mqa(nc, m, d, "cond2_0", w, False)


def stage_cond2_1(nc, m, d):
    w = Parts()
    w.wq = d["L1_cond2_Wq"]
    w.wkv = d["L1_cond2_Wkv"]
    w.wo = d["L1_cond2_Wo"]
    w.g_in = d["L1_cond2_g_in"]
    w.g_out = d["L1_cond2_g_out"]
    w.null_bias = d["L1_cond2_null_attn_bias"]
    w.mask = d["mask_bk0"]
    stage_mqa(nc, m, d, "cond2_1", w, False)


def stage_ffn0(nc, m, d):
    F = 1024
    FC = F // P
    LIMIT = 127.0
    r = m.R
    G = m.sb("ffn0_g", [P, FC, B * S], F32, r)
    w1 = m.sb("ffn0_w1", [P, DC, F], F32, r)
    w2 = m.sb("ffn0_w2", [P, FC, D], F32, r + 8192)
    wr = m.sb("ffn0_wr", [P, DC * F], F32, r + 16384)
    wide = m.sb("ffn0_wide", [P, NT, P], F32, r + 24576)
    XQ = m.sb("ffn0_xq", [P, NT, D], BF16, r + 32768)
    r += 65536
    w1q = m.sb("ffn0_w1q", [P, DC, F], BF16, r)
    w2q = m.sb("ffn0_w2q", [P, FC, D], BF16, r + 4096)
    XQT = m.sb("ffn0_xqt", [P, DC, B * S], BF16, r + 8192)
    RT = m.sb("ffn0_rt", [P, B * S], F32, r + 16384)
    r += 24576
    raw = [m.sb(f"ffn0_raw{i}", [P, B, S + 2], F32, r + i * 8224) for i in range(2)]
    r += 2 * 8224
    conv = [m.sb(f"ffn0_conv{i}", [P, B, S], F32, r + i * 8192) for i in range(2)]
    HF = [m.sb(f"ffn0_hf{i}", [P, F], F32, r + i * 4096) for i in range(2)]
    HQ = [m.sb(f"ffn0_hq{i}", [P, F], BF16, r + 8192 + i * 2048) for i in range(2)]
    HQT = [m.sb(f"ffn0_hqt{i}", [P, FC, P], BF16, r + 12288 + i * 2048) for i in range(2)]
    r += 16384
    taps = m.sb("ffn0_taps", [P, FC, 3], F32, r)
    bias = m.sb("ffn0_bias", [P, FC], F32, r + 96)
    wsum = m.sb("ffn0_wsum", [P, 8], F32, r + 128)
    wmean = m.sb("ffn0_wmean", [P, 8], F32, r + 160)
    wscale = m.sb("ffn0_wscale", [P, 8], F32, r + 192)
    cs = m.sb("ffn0_cs", [P, NT], F32, r + 224)
    cinv = m.sb("ffn0_cinv", [P, NT], F32, r + 288)
    less = m.sb("ffn0_less", [P, 8], F32, r + 352)
    hs = [m.sb(f"ffn0_hs{i}", [P, 8], F32, r + 384 + 32 * i) for i in range(2)]
    hinv = [m.sb(f"ffn0_hinv{i}", [P, 8], F32, r + 448 + 32 * i) for i in range(2)]

    loaded, taps_loaded, steps, summed, rowed, scaled, turned, freed, spread, spread_sb = (
        m.sem("ffn0_" + s) for s in ("loaded", "taps_loaded", "steps", "summed", "rounded", "scales_wide", "turned", "freed",
                                     "spread", "spread_sb"))
    with nc.Block() as block:
        @block.sync
        def _(sp):
            sp.dma_start(w1[:, :, :], d["ffn0_w1_t"].rearrange("(c p) f -> p c f", p=P)).then_inc(loaded, 16)
            sp.dma_start(w2[:, :, :], d["ffn0_w2_t"].rearrange("(c p) f -> p c f", p=P)).then_inc(loaded, 16)
            sp.dma_start(taps[:, :, :], d["ffn0_taps"].rearrange("(c p) k -> p c k", p=P)).then_inc(taps_loaded, 16)
            sp.dma_start(bias[:, :], d["ffn0_conv_b"]).then_inc(taps_loaded, 16)

        @block.gpsimd
        def _(pool):
            for i in range(2):
                nc.gpsimd.memset(raw[i][:, :, 0:1], 0.0)
                nc.gpsimd.memset(raw[i][:, :, S + 1:S + 2], 0.0)
            nc.gpsimd.memset(less[:, :], -ROUND)

        @block.vector
        def _(dve):
            n = [0]

            def step(ins):
                n[0] += 1
                ins.then_inc(steps, 1)
                dve.wait_ge(steps, n[0])

            step(nc.vector.tensor_reduce(cs[:, :], m.Y[:, :, :], AX.X, ALU.max, apply_absolute_value=True))
            step(nc.vector.tensor_scalar(cs[:, :], cs[:, :], 1e-5, None, ALU.max))
            step(nc.vector.reciprocal(cs[:, :], cs[:, :]))
            step(nc.vector.tensor_scalar(cs[:, :], cs[:, :], LIMIT, None, ALU.mult))
            for t in range(NT):
                last = nc.vector.tensor_scalar(m.Y[:, t, :], m.Y[:, t, :], cs[:, t:t + 1], ROUND, ALU.mult, ALU.add)
            step(last)
            nc.vector.tensor_scalar(XQ[:, :, :], m.Y[:, :, :], ROUND, None, ALU.subtract).then_inc(rowed, 1)
            step(nc.vector.reciprocal(cinv[:, :], cs[:, :]))
            dve.wait_ge(loaded, 32)
            step(nc.vector.tensor_reduce(wsum[:, 0:1], w1[:, :, :], AX.XY, ALU.add, apply_absolute_value=True))
            step(nc.vector.tensor_reduce(wsum[:, 1:2], w2[:, :, :], AX.XY, ALU.add, apply_absolute_value=True))
            n_sums = n[0]
            assert n_sums == WEIGHT_SUMS
            dve.wait_ge(summed, 1)
            step(nc.vector.tensor_scalar(wmean[:, 0:2], m.O[0][:, 0:2], 1.0 / (F * D), 1e-5, ALU.mult, ALU.max))
            step(nc.vector.reciprocal(wscale[:, 0:2], wmean[:, 0:2]))
            for j, (w, q) in enumerate(((w1, w1q), (w2, w2q))):
                flat = w[:, :, :].rearrange("p a b -> p (a b)")
                step(nc.vector.tensor_scalar(wr[:, :], flat, wscale[:, j:j + 1], ROUND, ALU.mult, ALU.add))
                step(nc.vector.tensor_scalar(wr[:, :], wr[:, :], ROUND, 1.0, ALU.subtract, ALU.min))
                step(nc.vector.tensor_scalar(q[:, :, :].rearrange("p a b -> p (a b)"), wr[:, :], -1.0, None, ALU.max))
            step(nc.vector.tensor_scalar(cinv[:, :], cinv[:, :], wmean[:, 0:1], None, ALU.mult))
            nc.vector.tensor_copy(wide[:, :, :], cinv[:, :].unsqueeze(2).broadcast_to([P, NT, P])).then_inc(scaled, 1)

        @block.tensor
        def _(pe):
            pe.wait_ge(rowed, 1)
            for j in range(2 * NG):
                g, c = divmod(j, DC)
                if j >= 2:
                    pe.wait_ge(freed, j - 1)
                bank = m.T[j % 2][:, 0:GRP // 2].bitcast(BF16)
                for t in range(4):
                    last = nc.tensor.transpose(bank[:, t * P:(t + 1) * P], XQ[:, 4 * g + t, c * P:(c + 1) * P], m.identb[:, :])
                last.then_inc(turned, 1)
            pe.wait_ge(steps, WEIGHT_SUMS)
            nc.tensor.matmul(m.O[0][:, 0:2], m.ones[:, :], wsum[:, 0:2], start=True, stop=True).then_inc(summed, 1)
            pe.wait_ge(scaled, 1)
            for t in range(NT):
                last = nc.tensor.matmul(m.SH[t // 4][:, (t % 4) * P:(t % 4 + 1) * P], wide[:, t, :], m.ident[:, :],
                                        start=True, stop=True)
                if t % 4 == 3:
                    last.then_inc(spread, 1)

        @block.scalar
        def _(act):
            for j in range(2 * NG):
                g, c = divmod(j, DC)
                act.wait_ge(turned, j + 1)
                nc.scalar.copy(XQT[:, c, g * GRP:(g + 1) * GRP], m.T[j % 2][:, 0:GRP // 2].bitcast(BF16)).then_inc(freed, 1)
            for g in range(NG):
                act.wait_ge(spread, g + 1)
                nc.scalar.copy(RT[:, g * GRP:(g + 1) * GRP], m.SH[g]).then_inc(spread_sb, 1)

    upped, rawed, convd, smooth = (m.sem("ffn0_" + s) for s in ("upped", "raw", "convolved", "smooth"))
    with nc.Block() as block:
        @block.tensor
        def _(pe):
            for f in range(FC):
                for g in range(NG):
                    if f:
                        pe.wait_ge(rawed, (f - 1) * NG + g + 1)
                    for c in range(DC):
                        last = nc.tensor.matmul(m.SH[g], w1q[:, c, f * P:(f + 1) * P], XQT[:, c, g * GRP:(g + 1) * GRP],
                                                start=(c == 0), stop=(c == DC - 1))
                    last.then_inc(upped, 1)

        @block.vector
        def _(dve):
            dve.wait_ge(taps_loaded, 32)
            for f in range(FC):
                z, a = raw[f % 2], conv[f % 2]
                for g in range(NG):
                    b, o = divmod(g * GRP, S)
                    dve.wait_ge(upped, f * NG + g + 1)
                    nc.vector.tensor_tensor(z[:, b, 1 + o:1 + o + GRP], m.SH[g], RT[:, g * GRP:(g + 1) * GRP],
                                            ALU.mult).then_inc(rawed, 1)
                dve.wait_ge(rawed, (f + 1) * NG)
                if f >= 2:
                    dve.wait_ge(smooth, f - 1)
                nc.vector.tensor_scalar(a[:, :, :], z[:, :, 1:S + 1], taps[:, f, 1:2], bias[:, f:f + 1],
                                        ALU.mult, ALU.add).then_inc(convd, 1)
                for k, tap in ((1, 0), (2, 2)):
                    dve.wait_ge(convd, 3 * f + k)
                    nc.vector.scalar_tensor_tensor(a[:, :, :], z[:, :, tap:tap + S], taps[:, f, tap:tap + 1], a[:, :, :],
                                                   ALU.mult, ALU.add).then_inc(convd, 1)

        @block.scalar
        def _(act):
            for f in range(FC):
                act.wait_ge(convd, 3 * f + 3)
                nc.scalar.activation(G[:, f, :], conv[f % 2][:, :, :].rearrange("p b s -> p (b s)"), ACT.Silu).then_inc(smooth, 1)

    back, steps2, quant, whole, turned2, freed2, ready, added = (
        m.sem("ffn0_" + s) for s in ("back", "steps2", "quant", "whole", "turned2", "freed2", "ready", "added"))
    with nc.Block() as block:
        @block.tensor
        def _(pe):
            def to_tokens(t):
                if t >= 2:
                    pe.wait_ge(quant, t - 1)
                for f in range(FC):
                    last = nc.tensor.transpose(m.S[t % 2][:, f * P:(f + 1) * P], G[:, f, t * P:(t + 1) * P], m.ident[:, :])
                last.then_inc(back, 1)

            def to_features(t):
                pe.wait_ge(whole, t + 1)
                if t >= 2:
                    pe.wait_ge(freed2, t - 1)
                bank = m.T[t % 2][:, :].bitcast(BF16)
                for f in range(FC):
                    last = nc.tensor.transpose(bank[:, f * P:(f + 1) * P], HQ[t % 2][:, f * P:(f + 1) * P], m.identb[:, :])
                last.then_inc(turned2, 1)

            def down(t):
                pe.wait_ge(freed2, t + 1)
                if t >= 2:
                    pe.wait_ge(added, t - 1)
                for f in range(FC):
                    last = nc.tensor.matmul(m.O[t % 2][:, 0:D], HQT[t % 2][:, f, :], w2q[:, f, :],
                                            start=(f == 0), stop=(f == FC - 1))
                last.then_inc(ready, 1)

            to_tokens(0)
            for t in range(NT):
                if t + 1 < NT:
                    to_tokens(t + 1)
                to_features(t)
                if t:
                    down(t - 1)
            down(NT - 1)

        @block.vector
        def _(dve):
            def quantise(t):
                i, n = t % 2, 6 * t
                dve.wait_ge(back, t + 1)
                nc.vector.tensor_reduce(hs[i][:, 0:1], m.S[i][:, :], AX.X, ALU.max, apply_absolute_value=True).then_inc(steps2, 1)
                dve.wait_ge(steps2, n + 1)
                nc.vector.tensor_scalar(hs[i][:, 1:2], hs[i][:, 0:1], 1e-5, None, ALU.max).then_inc(steps2, 1)
                dve.wait_ge(steps2, n + 2)
                nc.vector.reciprocal(hs[i][:, 2:3], hs[i][:, 1:2]).then_inc(steps2, 1)
                dve.wait_ge(steps2, n + 3)
                nc.vector.tensor_scalar(hs[i][:, 3:4], hs[i][:, 2:3], LIMIT, None, ALU.mult).then_inc(steps2, 1)
                dve.wait_ge(steps2, n + 4)
                if t >= 2:
                    dve.wait_ge(whole, t - 1)
                nc.vector.tensor_scalar(HF[i][:, :], m.S[i][:, :], hs[i][:, 3:4], ROUND, ALU.mult, ALU.add).then_inc(quant, 1)
                nc.vector.reciprocal(hinv[i][:, 0:1], hs[i][:, 3:4]).then_inc(steps2, 1)
                dve.wait_ge(steps2, n + 5)
                nc.vector.tensor_scalar(hinv[i][:, 1:2], hinv[i][:, 0:1], wmean[:, 1:2], None, ALU.mult).then_inc(steps2, 1)

            def add(t):
                dve.wait_ge(ready, t + 1)
                dve.wait_ge(steps2, 6 * t + 6)
                nc.vector.scalar_tensor_tensor(m.X[:, t, :], m.O[t % 2][:, 0:D], hinv[t % 2][:, 1:2], m.X[:, t, :],
                                               ALU.mult, ALU.add).then_inc(added, 1)

            quantise(0)
            for t in range(1, NT):
                if t >= 2:
                    add(t - 2)
                quantise(t)
            add(NT - 2)
            add(NT - 1)

        @block.scalar
        def _(act):
            for t in range(NT):
                act.wait_ge(quant, t + 1)
                if t >= 2:
                    act.wait_ge(turned2, t - 1)
                nc.scalar.activation(HQ[t % 2][:, :], HF[t % 2][:, :], ACT.Identity, bias=less[:, 0:1]).then_inc(whole, 1)
                act.wait_ge(turned2, t + 1)
                if t >= 2:
                    act.wait_ge(ready, t - 1)
                nc.scalar.copy(HQT[t % 2][:, :, :].rearrange("p f q -> p (f q)"), m.T[t % 2][:, :].bitcast(BF16)).then_inc(freed2, 1)


WEIGHT_SUMS = 8


def stage_distance(nc, m, d):
    PT_ = S // P
    r = m.R
    HB = m.sb("dist_h", [P, PT_, D], F32, r)
    HT = m.sb("dist_ht", [P, DC, S], F32, r + 8192)
    r += 16384
    rows = [m.sb(f"dist_row{i}", [P, D], F32, r + i * 1024) for i in range(5)]
    w0, b0, g0, b1, g1 = rows
    r += 5 * 1024
    w1 = m.sb("dist_w1", [P, DC, D], F32, r)
    w2 = m.sb("dist_w2", [P, DC, HEADS], F32, r + 2048)
    b2 = m.sb("dist_b2", [HEADS, 8], F32, r + 2176)
    far = m.sb("dist_pos", [P, PT_], F32, r + 2208)
    out = m.sb("dist_out", [HEADS, S + P], F32, r + 2240)
    r += 2240 + (S + P) * 4
    loaded, made, posed = m.sem("dist_loaded"), m.sem("dist_made"), m.sem("dist_posed")
    with nc.Block() as block:
        @block.sync
        def _(sp):
            row = lambda v: v.rearrange("(a n) -> a n", a=1).broadcast_to([P, D])
            for dst, src in ((w0, d["L1_cond_w0"].rearrange("a n -> (a n)")), (b0, d["L1_cond_b0"]), (g0, d["L1_cond_g0"]),
                             (b1, d["L1_cond_b1"]), (g1, d["L1_cond_g1"])):
                sp.dma_start(dst[:, :], row(src)).then_inc(loaded, 16)
            sp.dma_start(w1[:, :, :], d["L1_cond_w1"].rearrange("(c p) n -> p c n", p=P)).then_inc(loaded, 16)
            sp.dma_start(w2[:, :, :], d["L1_cond_w2"].rearrange("(c p) n -> p c n", p=P)).then_inc(loaded, 16)
            sp.dma_start(b2[:, 0:1], d["L1_cond_b2"].rearrange("(n a) -> n a", a=1)).then_inc(loaded, 16)

        @block.gpsimd
        def _(pool):
            nc.gpsimd.iota(far[:, :], pattern=[[P, PT_]], base=0, channel_multiplier=1,
                           allow_small_or_imprecise_dtypes=True).then_inc(made, 1)
            nc.gpsimd.memset(out[:, 0:P], FAR)

        @block.vector
        def _(dve):
            dve.wait_ge(loaded, 128)
            dve.wait_ge(made, 1)
            for t in range(PT_):
                nc.vector.scalar_tensor_tensor(HB[:, t, :], w0[:, :], far[:, t:t + 1], b0[:, :], ALU.mult, ALU.add).then_inc(posed, 1)

    stage_norm_turn(nc, m, "dist_n0", HB, HB, HT, g0, (loaded, 128), r, PT_, True)
    mixed, mixed_sb = m.sem("dist_mixed"), m.sem("dist_mixed_sb")
    with nc.Block() as block:
        @block.tensor
        def _(pe):
            for t in range(PT_):
                if t >= 4:
                    pe.wait_ge(mixed_sb, t - 3)
                for c in range(DC):
                    last = nc.tensor.matmul(m.SH[t % 4][:, 0:D], HT[:, c, t * P:(t + 1) * P], w1[:, c, :],
                                            start=(c == 0), stop=(c == DC - 1))
                last.then_inc(mixed, 1)

        @block.vector
        def _(dve):
            for t in range(PT_):
                dve.wait_ge(mixed, t + 1)
                nc.vector.tensor_tensor(HB[:, t, :], m.SH[t % 4][:, 0:D], b1[:, :], ALU.add).then_inc(mixed_sb, 1)

    stage_norm_turn(nc, m, "dist_n1", HB, HB, HT, g1, (loaded, 128), r, PT_, True)
    headed, headed_sb, stored = m.sem("dist_headed"), m.sem("dist_headed_sb"), m.sem("dist_stored")
    with nc.Block() as block:
        @block.tensor
        def _(pe):
            for g in range(S // GRP):
                for c in range(DC):
                    last = nc.tensor.matmul(m.SH[g][0:HEADS, :], w2[:, c, :], HT[:, c, g * GRP:(g + 1) * GRP],
                                            start=(c == 0), stop=(c == DC - 1))
                last.then_inc(headed, 1)

        @block.vector
        def _(dve):
            for g in range(S // GRP):
                dve.wait_ge(headed, g + 1)
                nc.vector.tensor_scalar(out[:, P + g * GRP:P + (g + 1) * GRP], m.SH[g][0:HEADS, :], b2[:, 0:1], None,
                                        ALU.add).then_inc(headed_sb, 1)

        @block.sync
        def _(sp):
            sp.wait_ge(headed_sb, S // GRP)
            sp.dma_start(d["distance"], out[:, :]).then_inc(stored, 16)
            sp.wait_ge(stored, 16)


def stage_cond1(nc, m, d):
    stage_distance(nc, m, d)
    w = Parts()
    w.wq = d["L1_cond_Wq"]
    w.wkv = d["L1_cond_Wkv"]
    w.wo = d["L1_cond_Wout"]
    w.g_in = d["L1_cond_g_norm"]
    w.g_out = d["L1_cond_g_out"]
    w.null_bias = d["L1_cond_null_attn_bias"]
    w.mask = d["mask_bf1"]
    w.q_scale = d["L1_cond_q_scale"]
    w.k_scale = d["L1_cond_k_scale"]
    stage_mqa(nc, m, d, "cond1", w, True)


def stage_attn1(nc, m, d):
    DK = 128
    at = m.R + 65536
    QT = m.sb("attn1_qt", [P, B * S], F32, at)
    KT = m.sb("attn1_kt", [P, B * S], F32, at + 8192)
    V = m.sb("attn1_v", [P, NT, DK], F32, at + 16384)
    causal = m.sb("attn1_causal", [P, S], F32, at + 24576)
    wq, wk, wv = (m.sb(f"attn1_w{n}", [P, DC, DK], F32, at + 28672 + i * 1024) for i, n in enumerate("qkv"))
    at += 32768
    loaded, made, projected, q_taken, k_taken, valued, v_taken = (
        m.sem("attn1_" + s) for s in ("loaded", "made", "projected", "q_taken", "k_taken", "valued", "v_taken"))
    stage_turn(nc, m, "attn1_in", m.Y, m.XT)
    with nc.Block() as block:
        @block.sync
        def _(sp):
            for dst, src in ((wq, d["L1_attn_Wq"]), (wk, d["L1_attn_Wk"]), (wv, d["L1_attn_Wv"])):
                sp.dma_start(dst[:, :, :], src.rearrange("(c p) n -> p c n", p=P)).then_inc(loaded, 16)

        @block.gpsimd
        def _(pool):
            nc.gpsimd.memset(causal[:, :], 0.0).then_inc(made, 1)
            pool.wait_ge(made, 1)
            nc.gpsimd.affine_select(out=causal[:, :], in_=causal[:, :], compare_op=ALU.is_ge, fill=FAR,
                                    base=S - P, pattern=[[-1, S]], channel_multiplier=1)

        @block.tensor
        def _(pe):
            pe.wait_ge(loaded, 48)
            for j in range(2 * NG):
                g, w, taken = j // 2, (wq, wk)[j % 2], (q_taken, k_taken)[j % 2]
                if j >= 4:
                    pe.wait_ge(taken, j // 2 - 1)
                for c in range(DC):
                    last = nc.tensor.matmul(m.SH[j % 4], w[:, c, :], m.XT[:, c, g * GRP:(g + 1) * GRP],
                                            start=(c == 0), stop=(c == DC - 1))
                last.then_inc(projected, 1)
            for t in range(NT):
                if t >= 4:
                    pe.wait_ge(v_taken, t - 3)
                for c in range(DC):
                    last = nc.tensor.matmul(m.TO[t % 4][:, 0:DK], m.XT[:, c, t * P:(t + 1) * P], wv[:, c, :],
                                            start=(c == 0), stop=(c == DC - 1))
                last.then_inc(valued, 1)

        @block.scalar
        def _(act):
            for g in range(NG):
                act.wait_ge(projected, 2 * g + 1)
                nc.scalar.mul(QT[:, g * GRP:(g + 1) * GRP], m.SH[(2 * g) % 4], float(DK) ** -0.5).then_inc(q_taken, 1)

        @block.vector
        def _(dve):
            for g in range(NG):
                dve.wait_ge(projected, 2 * g + 2)
                nc.vector.tensor_copy(KT[:, g * GRP:(g + 1) * GRP], m.SH[(2 * g + 1) % 4]).then_inc(k_taken, 1)
            for t in range(NT):
                dve.wait_ge(valued, t + 1)
                nc.vector.tensor_copy(V[:, t, :], m.TO[t % 4][:, 0:DK]).then_inc(v_taken, 1)

    nothing = lambda engine, it: None
    a = Parts()
    a.name = "attn1"
    a.iters = 1
    a.heads = 1
    a.per_head = 2
    a.units = causal_units(2)
    a.null = False
    a.at = at
    a.sync = None
    a.pool_first = None
    a.pool_bias = None
    a.bias_ready = None
    a.tensor_first = nothing
    a.scalar_first = nothing
    a.vector_first = nothing
    a.scores = lambda h, b, q: QT[:, b * S + q * P:b * S + (q + 1) * P]
    a.keys = lambda h, b, lo, hi: KT[:, b * S + lo:b * S + hi]
    a.values = lambda h, b, kb: V[:, b * QB + kb, :]
    a.bias = lambda h, b, q, L: causal[:, S - L:S]
    a.output = lambda it, b, q0: m.OT[:, 0, b * S + q0 * P:b * S + (q0 + 2) * P]
    stage_attention(nc, m, d, a)
    w_out = m.sb("attn1_wo", [P, 1, D], F32, m.R + 65536)
    stage_project_out(nc, m, "attn1_out", 1, w_out, d["L1_attn_Wo"], None, m.X)


def stage_moe1(nc, m, d):
    E, F = 8, 1024
    FC = F // P
    r = m.R
    k = route_buffers(m, r, "moe1", E, E)
    r += ROUTE_BYTES
    wr = m.sb("moe1_wr", [P, DC, E], F32, r)
    b2 = m.sb("moe1_b2", [E, D], F32, r + 64)
    combt = m.sb("moe1_combt", [E, NT, P], F32, r + 64 + 1024)
    r += 64 + 1024 + 8192
    w1 = [m.sb(f"moe1_w1_{i}", [P, DC, F], F32, r + i * 16384) for i in range(2)]
    w2 = [m.sb(f"moe1_w2_{i}", [P, FC, D], F32, r + 8192 + i * 16384) for i in range(2)]
    r += 32768
    hid = [m.sb(f"moe1_hid{i}", [P, FC, GRP], F32, r + i * 16384) for i in range(2)]
    r += 32768
    b1 = [m.sb(f"moe1_b1_{i}", [P, FC], F32, r + i * 32) for i in range(2)]
    small, made, steps, exped, turned, freed, logits, tcomb, tcomb_sb, based, based_x = (
        m.sem("moe1_" + s) for s in ("small", "made", "steps", "exped", "turned", "freed", "logits", "tcomb", "tcomb_sb",
                                     "based", "based_x"))
    weights = [m.sem(f"moe1_weights{i}") for i in range(2)]

    def load(sp, e, i):
        sp.dma_start(w1[i][:, :, :], d["L1_ffn_W1"][bass.ds(e, 1)].rearrange("e (c p) f -> p (e c) f", p=P)).then_inc(weights[i], 16)
        sp.dma_start(w2[i][:, :, :], d["L1_ffn_W2"][bass.ds(e, 1)].rearrange("e (c p) f -> p (e c) f", p=P)).then_inc(weights[i], 16)
        sp.dma_start(b1[i][:, :], d["moe1_b1"][bass.ds(e, 1)].rearrange("e p c -> (e p) c")).then_inc(weights[i], 16)

    with nc.Block() as block:
        @block.sync
        def _(sp):
            sp.dma_start(wr[:, :, :], d["L1_ffn_Wr"].rearrange("(c p) e -> p c e", p=P)).then_inc(small, 16)
            sp.dma_start(b2[:, :], d["L1_ffn_b2"]).then_inc(small, 16)
            for i in range(2):
                load(sp, i, i)

        @block.gpsimd
        def _(pool):
            nc.gpsimd.iota(k.iota[:, :], pattern=[[1, 8]], base=0, channel_multiplier=0,
                           allow_small_or_imprecise_dtypes=True).then_inc(made, 1)

        @block.tensor
        def _(pe):
            turn_tensor(nc, pe, m, m.Y, turned, freed)
            pe.wait_ge(freed, DC * NG)
            pe.wait_ge(small, 32)
            for t in range(NT):
                for c in range(DC):
                    last = nc.tensor.matmul(m.O[0][:, t * E:(t + 1) * E], m.XT[:, c, t * P:(t + 1) * P], wr[:, c, :],
                                            start=(c == 0), stop=(c == DC - 1))
            last.then_inc(logits, 1)
            pe.wait_ge(steps, ROUTE_STEPS)
            for t in range(NT):
                last = nc.tensor.transpose(m.SH[t // 4][0:E, (t % 4) * P:(t % 4 + 1) * P], k.comb[:, t, :], m.ident[:, :])
            last.then_inc(tcomb, 1)
            pe.wait_ge(tcomb_sb, 4)
            for t in range(NT):
                if t >= 4:
                    pe.wait_ge(based_x, t - 3)
                nc.tensor.matmul(m.TO[t % 4][:, 0:D], combt[:, t, :], b2[:, :], start=True, stop=True).then_inc(based, 1)

        @block.scalar
        def _(act):
            turn_scalar(nc, act, m, m.XT, turned, freed)
            route_scalar(nc, act, k, steps, exped)
            act.wait_ge(tcomb, 1)
            for g in range(4):
                nc.scalar.copy(combt[:, 4 * g:4 * g + 4, :].rearrange("e t q -> e (t q)"), m.SH[g][0:E, :]).then_inc(tcomb_sb, 1)

        @block.vector
        def _(dve):
            dve.wait_ge(made, 1)
            dve.wait_ge(logits, 1)
            n = route_vector(nc, dve, m, k, m.O[0][:, 0:NT * E].rearrange("p (t e) -> p t e", e=E), 1.0, 0.0, E, steps, exped)
            assert n == ROUTE_STEPS
            for t in range(NT):
                dve.wait_ge(based, t + 1)
                nc.vector.tensor_tensor(m.X[:, t, :], m.X[:, t, :], m.TO[t % 4][:, 0:D], ALU.add).then_inc(based_x, 1)

    up, smooth, down, added = (m.sem("moe1_" + s) for s in ("up", "smooth", "down", "added"))
    JOBS, UPS, TILES = 2 * NG, 2 * NG * FC, 2 * NT
    with nc.Block() as block:
        @block.sync
        def _(sp):
            with sp.Fori(0, E // 2 - 1) as it:
                for i in range(2):
                    sp.wait_ge(down, it * TILES + (i + 1) * NT)
                    load(sp, 2 * it + 2 + i, i)

        @block.tensor
        def _(pe):
            def project_up(it, j):
                i, g = divmod(j, NG)
                if g == 0:
                    pe.wait_ge(weights[i], it * 48 + 48)
                for f in range(FC):
                    u = j * FC + f
                    if u >= 4:
                        pe.wait_ge(smooth, it * UPS + u - 3)
                    for c in range(DC):
                        last = nc.tensor.matmul(m.SH[u % 4], w1[i][:, c, f * P:(f + 1) * P], m.XT[:, c, g * GRP:(g + 1) * GRP],
                                                start=(c == 0), stop=(c == DC - 1))
                    last.then_inc(up, 1)

            def project_down(it, j):
                i, g = divmod(j, NG)
                pe.wait_ge(smooth, it * UPS + (j + 1) * FC)
                for t in range(4):
                    q = 4 * j + t
                    if q >= 4:
                        pe.wait_ge(added, it * TILES + q - 3)
                    for f in range(FC):
                        last = nc.tensor.matmul(m.TO[q % 4][:, 0:D], hid[j % 2][:, f, t * P:(t + 1) * P], w2[i][:, f, :],
                                                start=(f == 0), stop=(f == FC - 1))
                    last.then_inc(down, 1)

            with pe.Fori(0, E // 2) as it:
                project_up(it, 0)
                for j in range(1, JOBS):
                    project_up(it, j)
                    project_down(it, j - 1)
                project_down(it, JOBS - 1)
                pe.wait_ge(added, (it + 1) * TILES)

        @block.scalar
        def _(act):
            with act.Fori(0, E // 2) as it:
                for j in range(JOBS):
                    for f in range(FC):
                        u = j * FC + f
                        act.wait_ge(up, it * UPS + u + 1)
                        if f == 0 and j >= 2:
                            act.wait_ge(down, it * TILES + 4 * (j - 1))
                        nc.scalar.activation(hid[j % 2][:, f, :], m.SH[u % 4], ACT.Gelu,
                                             bias=b1[j // NG][:, f:f + 1]).then_inc(smooth, 1)
                act.wait_ge(down, (it + 1) * TILES)

        @block.vector
        def _(dve):
            with dve.Fori(0, E // 2) as it:
                for q in range(TILES):
                    i, t = divmod(q, NT)
                    dve.wait_ge(down, it * TILES + q + 1)
                    nc.vector.scalar_tensor_tensor(m.X[:, t, :], m.TO[q % 4][:, 0:D], k.comb[:, t, bass.ds(2 * it + i, 1)],
                                                   m.X[:, t, :], ALU.mult, ALU.add).then_inc(added, 1)

    stored = m.sem("out_stored")
    with nc.Block() as block:
        @block.sync
        def _(sp):
            sp.dma_start(d["out"].rearrange("b (t p) d -> p (b t) d", p=P), m.X[:, :, :]).then_inc(stored, 16)
            sp.wait_ge(stored, 16)


ROUTE_STEPS = 18


def memory(nc, ctx):
    m = Parts()
    m.sb = lambda name, shape, dt, at: nc.alloc_sbuf_tensor_at(name, shape, dt, offset=at)
    m.sem = lambda name: nc.alloc_semaphore(name=name)
    base = 16512
    m.X = m.sb("x_res", [P, NT, D], F32, base)
    m.ident = m.sb("ident", [P, P], F32, base + 16384)
    m.identb = m.sb("identb", [P, P], BF16, base + 16896)
    m.ones = m.sb("ones", [P, P], F32, base + 17152)
    m.XT = m.sb("feat", [P, DC, B * S], F32, base + 17664)
    m.YAT = base + 34048
    m.Y = m.sb("toks", [P, NT, D], F32, m.YAT)
    m.R = base + 50432
    m.OT = m.sb("attn_out", [P, 8, B * S], F32, m.R)
    psum = lambda name, shape: ctx.enter_context(nc.psum_tensor(name, shape, F32))
    m.S = [psum(f"ps_s{i}", [P, 1024]) for i in range(2)]
    m.T = [psum(f"ps_t{i}", [P, 512]) for i in range(2)]
    m.O = [psum(f"ps_o{i}", [P, 512]) for i in range(2)]
    m.SH = [m.S[i // 2][:, (i % 2) * 512:(i % 2 + 1) * 512] for i in range(4)]
    m.TO = [m.T[0], m.T[1], m.O[0], m.O[1]]
    return m


def program(nc, d, stages=None):
    with ExitStack() as ctx:
        m = memory(nc, ctx)
        every = [stage_setup, stage_moe0, stage_attn0, stage_cond2_0, stage_ffn0, stage_cond1, stage_attn1, stage_cond2_1, stage_moe1]
        for stage in every if stages is None else stages:
            with nc.cleanup_on_exit():
                stage(nc, m, d)


def lay_out(inp):
    a = dict(inp)

    def heads_padded(w, axis):
        w = np.moveaxis(w, axis, 0)
        out = np.zeros((16, 32) + w.shape[1:], w.dtype)
        out[:, :16] = w.reshape((16, 16) + w.shape[1:])
        return np.ascontiguousarray(np.moveaxis(out.reshape((512,) + w.shape[1:]), 0, axis))

    a["L0_cond_wt_t"] = a["L0_cond_wt"].T
    a["L0_cond_wg_t"] = a["L0_cond_wg"].T
    a["cond_t"] = a["cond_64"].T
    halves = lambda w: [w[:, :128][None], w[:, 128:][None]]
    a["moe0_gate"] = np.concatenate([a["L0_cond_w_gate"]] + halves(a["L0_cond_sw_gate"]))
    a["moe0_up"] = np.concatenate([a["L0_cond_w_up"]] + halves(a["L0_cond_sw_up"]))
    a["moe0_down"] = np.concatenate([a["L0_cond_w_down"], a["L0_cond_sw_down"].reshape(2, 128, 256)])
    a["mask_bk0"] = a["mask_BxS_bk0"]
    a["mask_bf1"] = a["mask_BxS_bf1"]
    a["attn0_wq"] = heads_padded(a["L0_attn_Wq"], 1)
    a["attn0_wk"] = heads_padded(a["L0_attn_Wkv"][:, :256], 1)
    a["attn0_wv"] = heads_padded(a["L0_attn_Wkv"][:, 256:], 1)
    a["attn0_wo"] = heads_padded(a["L0_attn_Wo"], 0)
    a["ffn0_w1_t"] = a["L0_ffn_w1"].T
    a["ffn0_w2_t"] = a["L0_ffn_w2"].T
    a["ffn0_taps"] = a["L0_ffn_conv_w"].reshape(1024, 3)
    a["ffn0_conv_b"] = a["L0_ffn_conv_b"].reshape(8, 128).T
    a["moe1_b1"] = a["L1_ffn_b1"].reshape(8, 8, 128).transpose(0, 2, 1)
    return a


def scratch(nc, d):
    d["distance"] = nc.dram_tensor("distance_bias", [HEADS, S + P], F32, kind="Internal").ap()


_INS = ["x", "cond_t", "L0_cond_wt_t", "L0_cond_wg_t", "moe0_gate", "moe0_up", "moe0_down",
        "attn0_wq", "attn0_wk", "attn0_wv", "attn0_wo", "fside_16xSxS_0", "cond_64", "mask_bk0", "mask_bf1",
        "L0_cond2_Wq", "L0_cond2_Wkv", "L0_cond2_Wo", "L0_cond2_g_in", "L0_cond2_g_out", "L0_cond2_null_attn_bias",
        "L1_cond2_Wq", "L1_cond2_Wkv", "L1_cond2_Wo", "L1_cond2_g_in", "L1_cond2_g_out", "L1_cond2_null_attn_bias",
        "ffn0_w1_t", "ffn0_w2_t", "ffn0_taps", "ffn0_conv_b",
        "L1_cond_g_norm", "L1_cond_Wq", "L1_cond_Wkv", "L1_cond_q_scale", "L1_cond_k_scale", "L1_cond_null_attn_bias",
        "L1_cond_w0", "L1_cond_b0", "L1_cond_g0", "L1_cond_w1", "L1_cond_b1", "L1_cond_g1", "L1_cond_w2", "L1_cond_b2",
        "L1_cond_Wout", "L1_cond_g_out", "L1_attn_Wq", "L1_attn_Wk", "L1_attn_Wv", "L1_attn_Wo",
        "L1_ffn_Wr", "L1_ffn_W1", "moe1_b1", "L1_ffn_W2", "L1_ffn_b2"]


def kernel(**inputs):
    import concourse.bacc as bacc
    from concourse.bass_utils import run_bass_kernel_spmd

    laid = lay_out({name: np.asarray(v) for name, v in inputs.items()})
    nc = bacc.Bacc("TRN2", target_bir_lowering=False, num_devices=1)
    arrays, d = {}, {}
    for name in _INS:
        a = np.ascontiguousarray(laid[name])
        arrays["in_" + name] = a
        d[name] = nc.dram_tensor("in_" + name, a.shape, mybir.dt.from_np(a.dtype), kind="ExternalInput").ap()
    d["out"] = nc.dram_tensor("out_0_dram", (B, S, D), F32, kind="ExternalOutput").ap()
    scratch(nc, d)
    program(nc, d)
    return run_bass_kernel_spmd(nc, [arrays], core_ids=[0]).results[0]["out_0_dram"]
```
